# Optimizing a Trainium2 kernel written in Bass

```python
import numpy as np
import jax
import jax.numpy as jnp

def _softmax(x, axis=-1):
    return jax.nn.softmax(x, axis=axis)

def _gelu(x):
    return jax.nn.gelu(x, approximate=True)

def _silu(x):
    return jax.nn.silu(x)

def _sigmoid(x):
    return jax.nn.sigmoid(x)

def _layernorm(x, axis=-1, eps=1e-05):
    m = jnp.mean(x, axis=axis, keepdims=True)
    v = jnp.var(x, axis=axis, keepdims=True)
    return (x - m) / jnp.sqrt(v + eps)

def _scatter_add(tgt, idx, src, axis=0):
    return tgt.at[idx].add(src)

def _segment_sum(src, seg, n):
    return jax.ops.segment_sum(src, seg, n)
kernel_name = 'mk_decoder_postln_d1_seqx_r4_83a4ff'

def setup_inputs(seed: int=0):
    np.random.seed(seed)
    _w = jnp.asarray

    def _rec_inputs():
        import jax
        import jax.numpy as jnp
        _rk = jax.random.key(seed)
        x = -0.0003929 + 0.9999 * jax.random.normal(jax.random.fold_in(_rk, 1), (32, 256, 256), jnp.float32)
        _lenS = 256 - jax.random.randint(jax.random.fold_in(_rk, 7), (32,), 0, max(1, 256 // 4) + 1, jnp.int32)
        _lenS2 = 120 - jax.random.randint(jax.random.fold_in(_rk, 8), (32,), 0, max(1, 120 // 4) + 1, jnp.int32)
        _ctx_1024P = jax.random.normal(jax.random.fold_in(_rk, 11), (32, 16, 256), jnp.float32)
        _ctx_1024c = jax.random.dirichlet(jax.random.fold_in(_rk, 511), 0.3 * jnp.ones((16,), jnp.float32), (32, 120))
        _ctx_1024t = jnp.einsum('bsk,bkd->bsd', _ctx_1024c, _ctx_1024P)
        _ctx_1024t = _ctx_1024t * jax.lax.rsqrt(jnp.mean(jnp.square(_ctx_1024t)) + 1e-12) * 0.953939
        ctx_1024 = 2.81802e-05 + 1.00001 * (_ctx_1024t + 0.3 * jax.random.normal(jax.random.fold_in(_rk, 611), (32, 120, 256), jnp.float32))
        return (x, ctx_1024)
    x, ctx_1024 = _rec_inputs()

    def _L0_attn_setup():
        import jax, jax.numpy as jnp
        import numpy as np
        N_BASIS = 128
        N_CHANNELS = 64
        DECAY_INIT = 3.0
        B, T, V = (4, 1024, 256)
        key = jax.random.key(seed)
        ks = jax.random.split(key, 6)
        std = 0.02
        return {'x': jax.random.normal(ks[0], (B, T, V), dtype=jnp.float32), 'basis': jax.random.normal(ks[1], (V, 2 * N_BASIS), dtype=jnp.float32), 'q_coeffs': jax.random.normal(ks[2], (N_CHANNELS, 2 * N_BASIS), dtype=jnp.float32) * std, 'k_coeffs': jax.random.normal(ks[3], (N_CHANNELS, 2 * N_BASIS), dtype=jnp.float32) * std, 'v_coeffs': jax.random.normal(ks[4], (N_CHANNELS, 2 * N_BASIS), dtype=jnp.float32) * std, 'o_coeffs': jax.random.normal(ks[5], (N_CHANNELS, 2 * N_BASIS), dtype=jnp.float32) * std, 'decay_logit': jnp.asarray(DECAY_INIT, dtype=jnp.float32), 'out_scale': jnp.asarray(0.1, dtype=jnp.float32)}
    _L0_attn_all = _L0_attn_setup()
    _L0_attn_in = {k: v for k, v in _L0_attn_all.items() if k in ('basis', 'q_coeffs', 'k_coeffs', 'v_coeffs', 'o_coeffs', 'decay_logit', 'out_scale')}
    del _L0_attn_all

    def _L0_xattn_setup():
        import jax, jax.numpy as jnp
        import numpy as np
        B, S, E = (8, 512, 256)
        EPS = 0.001

        def _layer_norm(x, gamma, beta):
            mu = jnp.mean(x, axis=-1, keepdims=True)
            var = jnp.mean(jnp.square(x - mu), axis=-1, keepdims=True)
            return gamma * (x - mu) * jax.lax.rsqrt(var + EPS) + beta

        def _attention(q_in, k_in, v_in, WQ, WK, WV, causal):
            Q = jnp.einsum('bse,ed->bsd', q_in, WQ)
            K = jnp.einsum('bse,ed->bsd', k_in, WK)
            V = jnp.einsum('bse,ed->bsd', v_in, WV)
            d = K.shape[-1]
            scores = jnp.einsum('bqd,bkd->bqk', Q, K) / jnp.sqrt(jnp.float32(d))
            if causal:
                qlen, klen = (scores.shape[-2], scores.shape[-1])
                mask = jnp.triu(jnp.ones((qlen, klen), bool), k=1)
                scores = jnp.where(mask[None], -jnp.inf, scores)
            p = jax.nn.softmax(scores, axis=-1)
            return jnp.einsum('bqk,bkd->bqd', p, V)
        key = jax.random.key(seed)
        ks = jax.random.split(key, 10)
        sc = 1.0 / np.sqrt(E)
        return {'inputs': jax.random.normal(ks[0], (B, S, E), jnp.float32), 'context': jax.random.normal(ks[1], (B, S, E), jnp.float32), 'Wq': jax.random.normal(ks[2], (E, E), jnp.float32) * sc, 'Wk': jax.random.normal(ks[3], (E, E), jnp.float32) * sc, 'Wv': jax.random.normal(ks[4], (E, E), jnp.float32) * sc, 'Wcq': jax.random.normal(ks[5], (E, E), jnp.float32) * sc, 'Wck': jax.random.normal(ks[6], (E, E), jnp.float32) * sc, 'Wcv': jax.random.normal(ks[7], (E, E), jnp.float32) * sc, 'gamma': jnp.ones((E,), jnp.float32), 'beta': jnp.zeros((E,), jnp.float32), 'W1': jax.random.normal(ks[8], (E, E), jnp.float32) * sc, 'b1': jnp.zeros((E,), jnp.float32)}
    _L0_xattn_all = _L0_xattn_setup()
    _L0_xattn_in = {k: v for k, v in _L0_xattn_all.items() if k in ('Wq', 'Wk', 'Wv', 'Wcq', 'Wck', 'Wcv', 'gamma', 'beta', 'W1', 'b1')}
    del _L0_xattn_all

    def _L0_ffn_setup():
        import jax, jax.numpy as jnp
        import numpy as np
        IN_F, OUT_F, BLOCK, NBLK = (256, 1024, 64, 16)
        TOPK = NBLK // 4
        key = jax.random.key(seed)
        ks = jax.random.split(key, 7)
        s = 1.0 / np.sqrt(IN_F)
        s2 = 1.0 / np.sqrt(OUT_F)
        return {'x': jax.random.normal(ks[0], (4, 1024, IN_F), jnp.float32), 'router_w': jax.random.uniform(ks[1], (NBLK, IN_F), jnp.float32, -s, s), 'router_b': jax.random.uniform(ks[2], (NBLK,), jnp.float32, -s, s), 'w1': jax.random.uniform(ks[3], (OUT_F, IN_F), jnp.float32, -s, s), 'b1': jax.random.uniform(ks[4], (OUT_F,), jnp.float32, -s, s), 'w2': jax.random.uniform(ks[5], (IN_F, OUT_F), jnp.float32, -s2, s2), 'b2': jax.random.uniform(ks[6], (IN_F,), jnp.float32, -s2, s2)}
    _L0_ffn_all = _L0_ffn_setup()
    _L0_ffn_in = {k: v for k, v in _L0_ffn_all.items() if k in ('router_w', 'router_b', 'w1', 'b1', 'w2', 'b2')}
    del _L0_ffn_all
    return {'x': x, 'ctx_1024': ctx_1024, 'L0_attn_basis': _L0_attn_in['basis'], 'L0_attn_q_coeffs': _L0_attn_in['q_coeffs'], 'L0_attn_k_coeffs': _L0_attn_in['k_coeffs'], 'L0_attn_v_coeffs': _L0_attn_in['v_coeffs'], 'L0_attn_o_coeffs': _L0_attn_in['o_coeffs'], 'L0_attn_decay_logit': _L0_attn_in['decay_logit'], 'L0_attn_out_scale': _L0_attn_in['out_scale'], 'L0_xattn_Wq': _L0_xattn_in['Wq'], 'L0_xattn_Wk': _L0_xattn_in['Wk'], 'L0_xattn_Wv': _L0_xattn_in['Wv'], 'L0_xattn_Wcq': _L0_xattn_in['Wcq'], 'L0_xattn_Wck': _L0_xattn_in['Wck'], 'L0_xattn_Wcv': _L0_xattn_in['Wcv'], 'L0_xattn_gamma': _L0_xattn_in['gamma'], 'L0_xattn_beta': _L0_xattn_in['beta'], 'L0_xattn_W1': _L0_xattn_in['W1'], 'L0_xattn_b1': _L0_xattn_in['b1'], 'L0_ffn_router_w': _L0_ffn_in['router_w'], 'L0_ffn_router_b': _L0_ffn_in['router_b'], 'L0_ffn_w1': _L0_ffn_in['w1'], 'L0_ffn_b1': _L0_ffn_in['b1'], 'L0_ffn_w2': _L0_ffn_in['w2'], 'L0_ffn_b2': _L0_ffn_in['b2']}

def reference(x, ctx_1024, L0_attn_basis, L0_attn_q_coeffs, L0_attn_k_coeffs, L0_attn_v_coeffs, L0_attn_o_coeffs, L0_attn_decay_logit, L0_attn_out_scale, L0_xattn_Wq, L0_xattn_Wk, L0_xattn_Wv, L0_xattn_Wcq, L0_xattn_Wck, L0_xattn_Wcv, L0_xattn_gamma, L0_xattn_beta, L0_xattn_W1, L0_xattn_b1, L0_ffn_router_w, L0_ffn_router_b, L0_ffn_w1, L0_ffn_b1, L0_ffn_w2, L0_ffn_b2):
    import jax
    import jax.numpy as jnp

    def _L0_attn_ref(x, basis, q_coeffs, k_coeffs, v_coeffs, o_coeffs, decay_logit, out_scale):
        import jax, jax.numpy as jnp
        import numpy as np
        N_BASIS = 128
        N_CHANNELS = 64
        DECAY_INIT = 3.0
        B, T, V = (4, 1024, 256)
        dtype = x.dtype
        q_w = (basis @ q_coeffs.T).astype(dtype)
        k_w = (basis @ k_coeffs.T).astype(dtype)
        v_w = (basis @ v_coeffs.T).astype(dtype)
        o_w = (basis @ o_coeffs.T).astype(dtype)
        queries = jnp.einsum('btv,vc->btc', x, q_w)
        keys = jnp.einsum('btv,vc->btc', x, k_w)
        values = jnp.einsum('btv,vc->btc', x, v_w)
        scores = jnp.einsum('btc,bsc->bts', queries, keys)
        decay = jax.nn.sigmoid(decay_logit)
        t = x.shape[1]
        pos = jnp.arange(t)
        diff = pos[None, :] - pos[:, None]
        causal_mask = diff > 0
        exponent = jnp.maximum(diff.astype(jnp.float32) - 1.0, 0.0)
        decay_weights = decay ** exponent * causal_mask.astype(jnp.float32)
        scores = scores * decay_weights.astype(dtype)[None]
        retrieved = jnp.einsum('bts,bsc->btc', scores, values)
        out = jnp.einsum('btc,vc->btv', retrieved, o_w) * out_scale.astype(dtype)
        return out

    def _L0_xattn_ref(inputs, context, Wq, Wk, Wv, Wcq, Wck, Wcv, gamma, beta, W1, b1):
        import jax, jax.numpy as jnp
        import numpy as np
        B, S, E = (8, 512, 256)
        EPS = 0.001

        def _layer_norm(x, gamma, beta):
            mu = jnp.mean(x, axis=-1, keepdims=True)
            var = jnp.mean(jnp.square(x - mu), axis=-1, keepdims=True)
            return gamma * (x - mu) * jax.lax.rsqrt(var + EPS) + beta

        def _attention(q_in, k_in, v_in, WQ, WK, WV, causal):
            Q = jnp.einsum('bse,ed->bsd', q_in, WQ)
            K = jnp.einsum('bse,ed->bsd', k_in, WK)
            V = jnp.einsum('bse,ed->bsd', v_in, WV)
            d = K.shape[-1]
            scores = jnp.einsum('bqd,bkd->bqk', Q, K) / jnp.sqrt(jnp.float32(d))
            if causal:
                qlen, klen = (scores.shape[-2], scores.shape[-1])
                mask = jnp.triu(jnp.ones((qlen, klen), bool), k=1)
                scores = jnp.where(mask[None], -jnp.inf, scores)
            p = jax.nn.softmax(scores, axis=-1)
            return jnp.einsum('bqk,bkd->bqd', p, V)
        a = _attention(inputs, inputs, inputs, Wq, Wk, Wv, causal=True) + inputs
        h = _layer_norm(a, gamma, beta)
        c = _attention(h, context, context, Wcq, Wck, Wcv, causal=False) + h
        h = _layer_norm(c, gamma, beta)
        f = jax.nn.relu(jnp.einsum('bse,ed->bsd', h, W1) + b1)
        out = _layer_norm(f + h, gamma, beta)
        return jax.nn.relu(out)

    def _L0_ffn_ref(x, router_w, router_b, w1, b1, w2, b2):
        import jax, jax.numpy as jnp
        import numpy as np
        IN_F, OUT_F, BLOCK, NBLK = (256, 1024, 64, 16)
        TOPK = NBLK // 4
        x_shape = x.shape
        xf = x.reshape(-1, IN_F)
        n = xf.shape[0]
        prob = jax.nn.softmax(xf @ router_w.T + router_b, axis=-1)
        _, idx = jax.lax.top_k(prob, TOPK)
        mask = jnp.zeros((n, NBLK), bool).at[jnp.arange(n)[:, None], idx].set(True)
        w1b = w1.reshape(NBLK, BLOCK, IN_F)
        b1b = b1.reshape(NBLK, BLOCK)
        h = jnp.einsum('nd,ibd->nib', xf, w1b) + b1b
        h = jnp.where(mask[:, :, None], h, jnp.zeros((), h.dtype))
        h = jax.nn.relu(h)
        w2b = w2.reshape(IN_F, NBLK, BLOCK)
        y = jnp.einsum('nib,dib->nd', jnp.where(mask[:, :, None], h, 0.0), w2b) + b2
        return y.reshape(x_shape)
    x = _layernorm(x + _L0_attn_ref(x, L0_attn_basis, L0_attn_q_coeffs, L0_attn_k_coeffs, L0_attn_v_coeffs, L0_attn_o_coeffs, L0_attn_decay_logit, L0_attn_out_scale), axis=-1)
    x = _layernorm(x + _L0_xattn_ref(x, ctx_1024, L0_xattn_Wq, L0_xattn_Wk, L0_xattn_Wv, L0_xattn_Wcq, L0_xattn_Wck, L0_xattn_Wcv, L0_xattn_gamma, L0_xattn_beta, L0_xattn_W1, L0_xattn_b1), axis=-1)
    x = _layernorm(x + _L0_ffn_ref(x, L0_ffn_router_w, L0_ffn_router_b, L0_ffn_w1, L0_ffn_b1, L0_ffn_w2, L0_ffn_b2), axis=-1)
    return x

_drawn_inputs = setup_inputs


def setup_inputs(seed=0):
    import zlib

    import numpy as np

    out = dict(_drawn_inputs(seed))
    spreads = {'L0_xattn_gamma': (1.0, 0.2), 'L0_xattn_beta': (0.0, 0.1), 'L0_xattn_b1': (0.0, 0.1)}
    factors = {'L0_ffn_b1': 8.0, 'L0_ffn_b2': 3.069}
    for name, (base, spread) in spreads.items():
        noise = np.random.default_rng([zlib.crc32(name.encode()), seed]).standard_normal(out[name].shape)
        drawn = base * np.exp(spread * noise) if base else spread * noise
        out[name] = jnp.asarray(drawn.astype(out[name].dtype))
    for name, factor in factors.items():
        out[name] = (out[name] * factor).astype(out[name].dtype)
    return out
```

```python
from contextlib import ExitStack

import concourse.bass as bass
from concourse import mybir

ALU = mybir.AluOpType
ACT = mybir.ActivationFunctionType
AX = mybir.AxisListType
F32 = mybir.dt.float32
F32R = mybir.dt.float32r
BF16 = mybir.dt.bfloat16

P = 128
BIG = 1e30
EPS_BLOCK = 1e-5
EPS_XATTN = 1e-3

ORDER = [
    ("zt", 2), ("h0", 4), ("x1t", 1), ("ln4", 3), ("qkv", 0), ("h1", 4), ("g", 1), ("cs", 2),
    ("ctx", 1), ("h2", 4), ("x2sum", 3), ("sc", 0), ("h3", 4), ("cpt", 2), ("v", 1), ("cpv", 2),
    ("ret", 0), ("ln5", 3), ("s", 1), ("out1", 0), ("y0", 4), ("pt", 1), ("ln3", 2), ("x2t", 3),
    ("y1", 4), ("pv", 1), ("lg", 3), ("ln6", 4), ("ln1", 0), ("z3t", 2), ("mt", 3), ("ln2", 1),
    ("w1", 2),
]


def decoder_kernel(nc, x, xT, ctxT, basisT, qcT, kcT, vcT, ocT, decay_logit, out_scale,
                   WqT, WkT, Wv, WcqT, WckT, Wcv, gamma, beta, gammaC, betaC, W1, b1, rwT, rb, w1T, fb1, w2T, fb2, out):
    NB, S, E = x.shape
    SC = ctxT.shape[2]
    KC = E // P
    TC = S // P
    CH = qcT.shape[1]
    FF = w1T.shape[1]
    FC = FF // P
    NBLK = rwT.shape[1]
    BLK = FF // NBLK
    TOPK = NBLK // 4
    assert S == 256 and E == 256 and FC == 8
    SCALE = float(E) ** -0.5
    LAG = max(lag for _, lag in ORDER)
    SENT = 4
    NE = NBLK + SENT

    ctx = ExitStack()
    with ctx:
        def sb(name, shape, dt=F32):
            return ctx.enter_context(nc.sbuf_tensor(name, shape, dt))

        def sem(name):
            return ctx.enter_context(nc.semaphore(name))

        def bank(name):
            return ctx.enter_context(nc.psum_tensor(name, [P, 512], F32))

        pA, pB, pV, pC, pD, pE = (bank(n) for n in ("pA", "pB", "pV", "pC", "pD", "pE"))
        pH = [bank("pH0"), bank("pH1")]

        ident = sb("ident", [P, P])
        ident_bf = sb("ident_bf", [P, P], BF16)
        causal_bf = sb("causal_bf", [P, P], BF16)
        dmask = sb("dmask", [P, 384])
        qkv_w = sb("qkv_w", [P, KC, 3 * CH])
        o_wT = sb("o_wT", [CH, E])
        M_hi, M_lo = sb("M_hi", [P, KC, E], F32R), sb("M_lo", [P, KC, E], F32R)
        Wv_hi, Wv_lo = sb("Wv_hi", [P, KC, E], F32R), sb("Wv_lo", [P, KC, E], F32R)
        McT = sb("McT", [P, KC, E])
        Wcv_sb = sb("Wcv_sb", [P, KC, E])
        W1_hi, W1_lo = sb("W1_hi", [P, KC, E], F32R), sb("W1_lo", [P, KC, E], F32R)
        w1_hi, w1_lo = sb("w1_hi", [P, KC, FF], F32R), sb("w1_lo", [P, KC, FF], F32R)
        w2_hi, w2_lo = sb("w2_hi", [P, FC, E], F32R), sb("w2_lo", [P, FC, E], F32R)
        rw_sb = sb("rw_sb", [P, KC, NBLK])
        rb_row = sb("rb_row", [P, TC, NBLK])
        g_row, be_row = sb("g_row", [P, TC, E]), sb("be_row", [P, TC, E])
        b1_row, b2_row = sb("b1_row", [P, TC, E]), sb("b2_row", [P, TC, E])
        g_col, be_col = sb("g_col", [P, KC]), sb("be_col", [P, KC])
        NX = NBLK + 3
        expand = sb("expand", [NX, FC, P], BF16)
        half, eps_block, eps_xattn = sb("half", [P, TC]), sb("eps_block", [P, TC]), sb("eps_xattn", [P, TC])

        work = sb("work", [P, 10, 512])

        def shared(n):
            return work[:, n, :].rearrange("p (a b) -> p a b", a=2)

        big1 = work[:, 0:4, :].rearrange("p n e -> p (n e)").rearrange("p (k f) -> p k f", k=KC)
        raw = {n: shared(4 + i) for i, n in enumerate("abcd")}
        basis_sb, coef = shared(8), shared(9)
        scal = sb("scal", [P, 8])
        be_wide = sb("be_wide", [P, KC, P])
        b1_parts = sb("b1_parts", [1, 3, FF], BF16)
        b1_rest = sb("b1_rest", [1, 2, FF])

        x_sb = [sb(f"x_sb{i}", [P, TC, E]) for i in range(2)]
        xT_sb = [sb(f"xT_sb{i}", [P, KC, S]) for i in range(2)]
        ctx_sb = [sb(f"ctx_sb{i}", [P, KC, SC]) for i in range(2)]
        qT, kT = sb("qT", [CH, S]), sb("kT", [CH, S])
        v_sb = sb("v_sb", [P, TC, CH])
        dsc = sb("dsc", [P, 384])
        ret = sb("ret", [CH, S])
        x1p = shared(0)
        x1 = [sb(f"x1_{i}", [P, TC, E]) for i in range(2)]
        x1c = [sb(f"x1c_{i}", [P, TC, E]) for i in range(2)]
        x1T = sb("x1T", [P, KC, S])
        x1T_hi, x1T_lo = sb("x1T_hi", [P, KC, S], F32R), sb("x1T_lo", [P, KC, S], F32R)
        G = shared(1)
        V = shared(2)
        pr = sb("pr", [P, 384])
        prT = sb("prT", [P, 384])
        nmax, ssum, rsum = sb("nmax", [P, TC]), sb("ssum", [P, TC]), sb("rsum", [P, TC])
        asum = shared(3)
        z2 = shared(8)
        hg = shared(4)
        h = [sb(f"h_{i}", [P, TC, E]) for i in range(2)]
        N_sb = [sb(f"N_sb{i}", [P, KC, SC]) for i in range(2)]
        Vc = [sb(f"Vc{i}", [P, E]) for i in range(2)]
        hT = sb("hT", [P, KC, S])
        prc = sb("prc", [P, TC, SC])
        prcT = sb("prcT", [P, S])
        nmaxc, ssumc, rsumc = sb("nmaxc", [P, TC]), sb("ssumc", [P, TC]), sb("rsumc", [P, TC])
        csum = shared(5)
        z3 = shared(6)
        h2g = shared(7)
        h2 = [sb(f"h2_{i}", [P, TC, E]) for i in range(2)]
        z3T_hi, z3T_lo = sb("z3T_hi", [P, KC, S], F32R), sb("z3T_lo", [P, KC, S], F32R)
        fpre = sb("fpre", [P, TC, E])
        fsum = sb("fsum", [P, TC, E])
        z4 = sb("z4", [P, TC, E])
        z4g, z4b = sb("z4g", [P, TC, E]), shared(9)
        x2p = sb("x2p", [P, TC, E])
        x2 = sb("x2", [P, TC, E])
        x2b = [sb(f"x2b_{i}", [P, TC, E]) for i in range(2)]
        x2T = sb("x2T", [P, KC, S])
        x2T_hi = [sb(f"x2T_hi{i}", [P, KC, S], F32R) for i in range(2)]
        x2T_lo = [sb(f"x2T_lo{i}", [P, KC, S], F32R) for i in range(2)]
        logit = sb("logit", [P, TC, NBLK])
        lmax = sb("lmax", [P, TC])
        prob = sb("prob", [P, TC, NE])
        top8 = sb("top8", [P, TC, 8])
        top4 = sb("top4", [P, TC, 8])
        struck = sb("struck", [P, TC, NE])
        nmask = sb("nmask", [P, TC, NBLK], BF16)
        maskT = [sb(f"maskT{i}", [NX, S], BF16) for i in range(2)]
        hid_hi, hid_lo = sb("hid_hi", [P, FC, S], F32R), sb("hid_lo", [P, FC, S], F32R)
        ysum = sb("ysum", [P, TC, E])
        o_sb = [sb(f"o_sb{i}", [P, TC, E]) for i in range(2)]
        LN = range(1, 7)
        st = {k: sb(f"st{k}", [P, TC, 6]) for k in LN}
        mv = {k: sb(f"mv{k}", [P, TC, 2]) for k in LN}
        ve = {k: sb(f"ve{k}", [P, TC]) for k in LN}
        rstd = {k: sb(f"rstd{k}", [P, TC]) for k in LN}

        s_ld, s_ld2, s_ld3 = sem("s_ld"), sem("s_ld2"), sem("s_ld3")
        s_c = {e: sem(f"s_c_{e}") for e in ("pool", "pe", "act", "dve", "dma")}
        s_chain = sem("s_chain")
        s_x = [sem(f"s_x{i}") for i in range(2)]
        s_xT = [sem(f"s_xT{i}") for i in range(2)]
        s_ctx = [sem(f"s_ctx{i}") for i in range(2)]
        s_st = [sem(f"s_st{i}") for i in range(2)]
        names = ("qkv_mm q k v sc_mm dsc ret_mm ret out1_mm x1p "
                 "ctx_mm N Vc x1t_mm x1T x1Th x1Tl g_mm G v_mm V s_mm smax ssum pt_mm prT rsum pv_mm asum hg h "
                 "zt_mm hT cs_mm cmax csm cpt_mm prcT rsumc cpv_mm csum h2g h2 x1c "
                 "z3t_mm z3h z3l w1_mm fpre fsum z4g z4b x2p x2b "
                 "x2t_mm x2T x2Th x2Tl lg_mm logit lmax prob top8 top4 struck nmask mt_mm maskT "
                 "y_mm ysum").split()
        s = {n: sem(f"s_{n}") for n in names}
        s_hmm = [sem(f"s_h_mm{f}") for f in range(4)]
        s_hhi = [sem(f"s_hid_hi{f}") for f in range(4)]
        s_hlo = [sem(f"s_hid_lo{f}") for f in range(4)]
        s_stat = {k: sem(f"s_stat{k}") for k in LN}
        s_mv = {k: sem(f"s_mv{k}") for k in LN}
        s_ve = {k: sem(f"s_ve{k}") for k in LN}
        s_rstd = {k: sem(f"s_rstd{k}") for k in LN}
        s_ln = {k: sem(f"s_ln{k}") for k in LN}

        def after(eng, which, n):
            if not isinstance(n, int) or n > 0:
                eng.wait_ge(which, n)

        def after_apart(eng, which, n, own):
            if not isinstance(n, int):
                n = eng.snap(n)
                eng.wait_ge(own, 1)
            after(eng, which, n)

        def loads(b, par):
            return 8 * (b - par) + 16

        def run(eng, steps, tail=None):
            def turn(i, par):
                for name, lag in ORDER:
                    b = i - lag
                    if name in steps and (not isinstance(b, int) or 0 <= b < NB):
                        steps[name](b, (par + lag) % 2)
                if tail:
                    tail(i, par)
            first = LAG + 2 + LAG % 2
            for i in range(first):
                turn(i, i % 2)
            with eng.Fori(first, NB - 1, 2) as i:
                turn(i, 0)
                turn(i + 1, 1)
            for i in range(NB, NB + LAG):
                turn(i, i % 2)

        def half_tile(t, c):
            return t[:, c, :]

        block = ctx.enter_context(nc.Block())

        @block.sync
        def _(sp):
            def rows(w):
                return w.rearrange("(k p) n -> p k n", p=P)

            def fetch(dst, src, landed=s_ld):
                sp.dma_start(dst, src).then_inc(landed, 16)

            fetch(basis_sb[:, :, :], rows(basisT))
            for n, w in enumerate((qcT, kcT, vcT, ocT)):
                fetch(coef[:, :, n * CH:(n + 1) * CH], rows(w))
            fetch(scal[:, 0:1], decay_logit.partition_broadcast(P))
            fetch(scal[:, 1:2], out_scale.partition_broadcast(P))
            for n, w in zip("abcd", (WqT, WkT, WcqT, WckT)):
                fetch(raw[n][:, :, :], rows(w))
            fetch(g_col[:, :], gammaC)
            fetch(be_col[:, :], betaC)
            for t in range(TC):
                fetch(g_row[:, t, :], gamma.partition_broadcast(P))
                fetch(be_row[:, t, :], beta.partition_broadcast(P))
                fetch(b1_row[:, t, :], b1.partition_broadcast(P))
                fetch(b2_row[:, t, :], fb2.partition_broadcast(P))
                fetch(rb_row[:, t, :], rb.partition_broadcast(P))
            fetch(Wcv_sb[:, :, :], rows(Wcv))
            fetch(rw_sb[:, :, :], rows(rwT))
            fetch(b1_rest[:, 0, :], fb1.rearrange("(o n) -> o n", o=1))
            fetch(big1[:, :, :], rows(w1T))
            sp.wait_ge(s_c["pe"], 3)
            fetch(raw["a"][:, :, :], rows(Wv), s_ld2)
            fetch(raw["b"][:, :, :], rows(W1), s_ld2)
            sp.wait_ge(s_c["dve"], 2)
            fetch(big1[:, :, :].rearrange("p k (c n) -> p (k c) n", n=E), rows(w2T), s_ld3)
            sp.wait_ge(s_c["dve"], 5)
            sp.wait_ge(s_c["pool"], 5)
            for n in range(3):
                sp.dma_start(expand[NBLK + n:NBLK + n + 1, :, :],
                             b1_parts[:, n, :].rearrange("o (c m) -> o c m", m=P)).then_inc(s_c["dma"], 16)

            def load(b, par):
                after(sp, s["x1p"], b - 1)
                sp.dma_start(x_sb[par][:, :, :], x[b].rearrange("(t p) e -> p t e", p=P)).then_inc(s_x[par], 16)
                after(sp, s["qkv_mm"], b - 1)
                sp.dma_start(xT_sb[par][:, :, :], xT[b].rearrange("(k p) t -> p k t", p=P)).then_inc(s_xT[par], 16)
                after(sp, s["ctx_mm"], b - 1)
                sp.dma_start(ctx_sb[par][:, :, :], ctxT[b].rearrange("(k p) t -> p k t", p=P)).then_inc(s_ctx[par], 16)

            def store(b, par):
                after(sp, s_ln[6], b + 1)
                sp.dma_start(out[b].rearrange("(t p) e -> p t e", p=P), o_sb[par][:, :, :]).then_inc(s_st[par], 16)

            lag = dict(ORDER)["ln6"]

            def turn(i, par):
                if not isinstance(i, int) or i < NB:
                    load(i, par)
                j = i - lag - 1
                if not isinstance(j, int) or 0 <= j < NB:
                    store(j, (par + lag + 1) % 2)

            first = LAG + 2 + LAG % 2
            for i in range(first):
                turn(i, i % 2)
            with sp.Fori(first, NB - 1, 2) as i:
                turn(i, 0)
                turn(i + 1, 1)
            for i in range(NB, NB + lag + 1):
                turn(i, i % 2)
            for par in range(2):
                sp.wait_ge(s_st[par], 16 * (NB // 2))

        N_LD = 16 * (1 + 4 + 2 + 4 + 2 + 5 * TC + 4)

        @block.gpsimd
        def _(pool):
            done = s_c["pool"]
            pool.memset(ident[:, :], 0.0).then_inc(done, 1)
            pool.memset(causal_bf[:, :], 0.0).then_inc(done, 1)
            pool.memset(expand[:, :, :], 1.0).then_inc(done, 1)
            pool.wait_ge(done, 3)
            pool.affine_select(out=ident[:, :], in_=ident[:, :], compare_op=ALU.not_equal, fill=1.0, base=0,
                               pattern=[[-1, P]], channel_multiplier=1).then_inc(done, 1)
            pool.affine_select(out=causal_bf[:, :], in_=causal_bf[:, :], compare_op=ALU.is_ge, fill=-BIG, base=0,
                               pattern=[[-1, P]], channel_multiplier=1).then_inc(done, 1)
            ex = expand[0:NBLK, :, :]
            pool.wait_ge(done, 5)
            pool.affine_select(out=ex, in_=ex, compare_op=ALU.is_ge, fill=0.0, base=0,
                               pattern=[[P, FC], [1, P]], channel_multiplier=-BLK).then_inc(done, 1)
            pool.wait_ge(done, 6)
            pool.affine_select(out=ex, in_=ex, compare_op=ALU.is_ge, fill=0.0, base=BLK - 1,
                               pattern=[[-P, FC], [-1, P]], channel_multiplier=BLK).then_inc(done, 1)
            pool.tensor_copy(ident_bf[:, :], ident[:, :]).then_inc(done, 1)
            pool.memset(half[:, :], -0.5).then_inc(done, 1)
            for par in range(2):
                pool.memset(maskT[par][:, :], 1.0).then_inc(done, 1)
            pool.memset(prob[:, :, :], -1.0).then_inc(done, 1)
            pool.memset(top4[:, :, :], -1.0).then_inc(done, 1)
            steps = x2p[:, :, :].rearrange("p t e -> p (t e)")[:, 0:384].bitcast(mybir.dt.int32)
            pool.iota(steps[:, 0:256], pattern=[[-1, 256]], base=P - 1, channel_multiplier=1).then_inc(done, 1)
            pool.iota(steps[:, 256:384], pattern=[[-1, P]], base=-1, channel_multiplier=1).then_inc(done, 1)
            pool.memset(scal[:, 2:3], 2.718281828459045).then_inc(done, 1)
            pool.memset(eps_block[:, :], EPS_BLOCK).then_inc(done, 1)
            pool.memset(eps_xattn[:, :], EPS_XATTN).then_inc(done, 1)
            pool.wait_ge(s_ld, N_LD)
            pool.wait_ge(done, 18)
            pool.tensor_scalar(scal[:, 3:4], scal[:, 0:1], -1.0, 0.0, ALU.mult, ALU.add).then_inc(done, 1)
            raised = x2[:, :, :].rearrange("p t e -> p (t e)")[:, 0:384]
            pool.tensor_copy(raised, steps).then_inc(done, 1)
            pool.wait_ge(done, 20)
            pool.tensor_tensor(scal[:, 4:5], scal[:, 2:3], scal[:, 3:4], ALU.pow).then_inc(done, 1)
            pool.wait_ge(s_c["dve"], 6)
            pool.tensor_tensor(dmask[:, :], fpre[:, :, :].rearrange("p t e -> p (t e)")[:, 0:384],
                               fsum[:, :, :].rearrange("p t e -> p (t e)")[:, 0:384], ALU.pow).then_inc(done, 1)
            pool.wait_ge(done, 22)
            pool.affine_select(out=dmask[:, 0:256], in_=dmask[:, 0:256], compare_op=ALU.is_ge, fill=0.0, base=P - 1,
                               pattern=[[-1, 256]], channel_multiplier=1).then_inc(done, 1)
            pool.affine_select(out=dmask[:, 256:384], in_=dmask[:, 256:384], compare_op=ALU.is_ge, fill=0.0, base=-1,
                               pattern=[[-1, P]], channel_multiplier=1).then_inc(done, 1)

            def norm_scale(k, b, eps):
                after(pool, s_mv[k], b + 1)
                pool.tensor_tensor(ve[k][:, :], mv[k][:, :, 1], eps[:, :], ALU.add).then_inc(s_ve[k], 1)
                after(pool, s_ve[k], b + 1)
                pool.tensor_tensor(rstd[k][:, :], ve[k][:, :], half[:, :], ALU.pow).then_inc(s_rstd[k], 1)

            def affine(z, zg, out_t, s_g, s_b, b):
                pool.tensor_tensor(zg[:, :, :], z[:, :, :], g_row[:, :, :], ALU.mult).then_inc(s_g, 1)
                after(pool, s_g, b + 1)
                pool.tensor_tensor(out_t[:, :, :], zg[:, :, :], be_row[:, :, :], ALU.add).then_inc(s_b, 1)

            def out1(b, par):
                norm_scale(1, b, eps_block)

            def pv(b, par):
                norm_scale(2, b, eps_xattn)

            def ln2(b, par):
                after(pool, s_ln[2], b + 1)
                after(pool, s["csum"], b - 1)
                affine(z2, hg, h[par], s["hg"], s["h"], b)

            def cpv(b, par):
                norm_scale(3, b, eps_xattn)

            def ln3(b, par):
                after(pool, s_ln[3], b + 1)
                after(pool, s["fsum"], b - 1)
                affine(z3, h2g, h2[par], s["h2g"], s["h2"], b)
                after_apart(pool, s_ln[1], b + 1, done)
                after(pool, s["x2p"], b - 1)
                pool.tensor_scalar(x1c[par][:, :, :], x1[par][:, :, :], 1.0, 0.0, ALU.mult, ALU.add)\
                    .then_inc(s["x1c"], 1)

            def w1(b, par):
                norm_scale(4, b, eps_xattn)

            def ln4(b, par):
                after(pool, s_ln[4], b + 1)
                after(pool, s["x2p"], b)
                affine(z4, z4g, z4b, s["z4g"], s["z4b"], b)

            def x2sum(b, par):
                norm_scale(5, b, eps_block)

            def ln5(b, par):
                after(pool, s_ln[5], b + 1)
                after(pool, s["ysum"], b - 1)
                pool.tensor_tensor(x2b[par][:, :, :], x2[:, :, :], b2_row[:, :, :], ALU.add).then_inc(s["x2b"], 1)

            def y(b, par):
                norm_scale(6, b, eps_block)

            run(pool, dict(out1=out1, pv=pv, ln2=ln2, cpv=cpv, ln3=ln3, w1=w1, ln4=ln4, x2sum=x2sum, ln5=ln5, y1=y))

        @block.tensor
        def _(pe):
            def product(out_ap, terms):
                for n, (lhs, rhs) in enumerate(terms):
                    mm = pe.matmul(out_ap, lhs, rhs, start=(n == 0), stop=(n == len(terms) - 1))
                return mm

            def split(lhs_hi, lhs_lo, rhs_hi, rhs_lo):
                return [(lhs_hi, rhs_hi), (lhs_hi, rhs_lo), (lhs_lo, rhs_hi)]

            def cols(c, n=P):
                return slice(c * n, (c + 1) * n)

            done = s_c["pe"]
            pe.wait_ge(s_ld, N_LD)
            for c in range(KC):
                product(pA[:, 192 * c:192 * c + 192],
                        [(basis_sb[:, k, cols(c)], coef[:, k, 0:3 * CH]) for k in range(KC)])
            product(pB[0:CH, 0:E], [(coef[:, k, 3 * CH:4 * CH], basis_sb[:, k, :]) for k in range(KC)]).then_inc(done, 1)
            for c in range(KC):
                mm = product(pC[:, cols(c, E)], [(raw["a"][:, k, cols(c)], raw["b"][:, k, :]) for k in range(KC)])
            mm.then_inc(done, 1)
            for c in range(KC):
                mm = product(pD[:, cols(c, E)], [(raw["d"][:, k, cols(c)], raw["c"][:, k, :]) for k in range(KC)])
            mm.then_inc(done, 1)
            pe.wait_ge(s_ld2, 32)
            pe.wait_ge(s_c["dve"], 1)
            product(pE[:, 0:E], [(be_wide[:, k, :], raw["b"][:, k, :]) for k in range(KC)]).then_inc(done, 1)
            pe.wait_ge(s_c["dve"], 10)
            pe.wait_ge(s_c["act"], 10)
            pe.wait_ge(s_c["pool"], 24)
            pe.wait_ge(s_c["dma"], 48)

            def qkv(b, par):
                pe.wait_ge(s_xT[par], loads(b, par))
                after(pe, s["x1p"], b)
                product(pA[:, 0:S], [(qkv_w[:, k, 0:2 * CH], xT_sb[par][:, k, :]) for k in range(KC)])
                for c in range(TC):
                    mm = product(pA[:, S + CH * c:S + CH * c + CH],
                                 [(xT_sb[par][:, k, cols(c)], qkv_w[:, k, 2 * CH:3 * CH]) for k in range(KC)])
                mm.then_inc(s["qkv_mm"], 1)

            def sc(b, par):
                after(pe, s["v"], b + 1)
                product(pA[:, 0:256], [(kT[:, P:S], qT[:, :])])
                product(pA[:, 256:384], [(kT[:, 0:P], qT[:, 0:P])]).then_inc(s["sc_mm"], 1)

            def ret_(b, par):
                after(pe, s["dsc"], b + 1)
                pe.matmul(pA[0:CH, 0:S], v_sb[:, 1, :], dsc[:, 0:256], start=True, stop=False)
                pe.matmul(pA[0:CH, 0:P], v_sb[:, 0, :], dsc[:, 256:384], start=False, stop=True)\
                    .then_inc(s["ret_mm"], 1)

            def out1(b, par):
                after(pe, s["ret"], b + 1)
                for c in range(TC):
                    mm = product(pA[:, cols(c, E)], [(ret[:, cols(c)], o_wT[:, :])])
                mm.then_inc(s["out1_mm"], 1)

            def ctx_(b, par):
                pe.wait_ge(s_ctx[par], loads(b, par))
                after(pe, s["V"], b)
                for c in range(KC):
                    product(pV[:, SC * c:SC * c + SC],
                            [(McT[:, k, cols(c)], ctx_sb[par][:, k, :]) for k in range(KC)])
                product(pV[0:SC, 256:512], [(ctx_sb[par][:, k, :], Wcv_sb[:, k, :]) for k in range(KC)])\
                    .then_inc(s["ctx_mm"], 1)

            def turned(bank_ap, src):
                for k in range(KC):
                    for c in range(TC):
                        mm = pe.transpose(bank_ap[:, S * k + P * c:S * k + P * c + P], src[:, c, cols(k)], ident[:, :])
                return mm

            def x1t(b, par):
                after(pe, s_ln[1], b + 1)
                after(pe, s["asum"], b)
                turned(pB, x1[par]).then_inc(s["x1t_mm"], 1)

            def g(b, par):
                after(pe, s["x1T"], b + 1)
                for c in range(KC):
                    terms = []
                    for k in range(KC):
                        terms += split(M_hi[:, k, cols(c)], M_lo[:, k, cols(c)], x1T_hi[:, k, :], x1T_lo[:, k, :])
                    mm = product(pB[:, cols(c, S)], terms)
                mm.then_inc(s["g_mm"], 1)

            def v(b, par):
                after(pe, s["x1Tl"], b + 1)
                after(pe, s["Vc"], b + 1)
                for c in range(TC):
                    terms = []
                    for k in range(KC):
                        terms += split(x1T_hi[:, k, cols(c)], x1T_lo[:, k, cols(c)], Wv_hi[:, k, :], Wv_lo[:, k, :])
                    mm = product(pV[:, cols(c, E)], terms)
                mm.then_inc(s["v_mm"], 1)

            def s_(b, par):
                after(pe, s["G"], b + 1)
                for k in range(KC):
                    pe.matmul(pB[:, 0:256], G[:, k, P:S], x1T[:, k, :], start=(k == 0), stop=False)
                pe.matmul(pB[:, P:256], ident_bf[:, :], causal_bf[:, :], start=False, stop=True)
                for k in range(KC):
                    pe.matmul(pB[:, 256:384], G[:, k, 0:P], x1T[:, k, 0:P], start=(k == 0), stop=False)
                pe.matmul(pB[:, 256:384], ident_bf[:, :], causal_bf[:, :], start=False, stop=True)\
                    .then_inc(s["s_mm"], 1)

            def pt(b, par):
                after(pe, s["ssum"], b + 1)
                for c in range(3):
                    mm = pe.transpose(pB[:, cols(c)], pr[:, cols(c)], ident[:, :])
                mm.then_inc(s["pt_mm"], 1)

            def pv(b, par):
                after(pe, s["prT"], b + 1)
                after(pe, s["V"], b + 1)
                product(pB[:, 0:256], [(prT[:, 256:384], V[:, 0, :])])
                product(pB[:, 256:512], [(prT[:, cols(c)], V[:, c, :]) for c in range(TC)]).then_inc(s["pv_mm"], 1)

            def zt(b, par):
                after(pe, s_ln[2], b + 1)
                after(pe, s["csum"], b)
                turned(pC, z2).then_inc(s["zt_mm"], 1)

            def cs(b, par):
                after(pe, s["hT"], b + 1)
                after(pe, s["N"], b + 1)
                for c in range(TC):
                    mm = product(pC[:, SC * c:SC * c + SC],
                                 [(hT[:, k, cols(c)], N_sb[par][:, k, :]) for k in range(KC)])
                mm.then_inc(s["cs_mm"], 1)

            def cpt(b, par):
                after(pe, s["csm"], b + 1)
                for c in range(TC):
                    mm = pe.transpose(pC[0:SC, cols(c)], prc[:, c, :], ident[:, :])
                mm.then_inc(s["cpt_mm"], 1)

            def cpv(b, par):
                after(pe, s["prcT"], b + 1)
                after(pe, s["Vc"], b + 1)
                for c in range(TC):
                    mm = product(pC[:, cols(c, E)], [(prcT[0:SC, cols(c)], Vc[par][0:SC, :])])
                mm.then_inc(s["cpv_mm"], 1)

            def z3t(b, par):
                after(pe, s_ln[3], b + 1)
                after(pe, s["fpre"], b)
                turned(pD, z3).then_inc(s["z3t_mm"], 1)

            def w1(b, par):
                after(pe, s["z3l"], b + 1)
                for c in range(TC):
                    terms = []
                    for k in range(KC):
                        terms += split(z3T_hi[:, k, cols(c)], z3T_lo[:, k, cols(c)], W1_hi[:, k, :], W1_lo[:, k, :])
                    mm = product(pD[:, cols(c, E)], terms)
                mm.then_inc(s["w1_mm"], 1)

            def x2t(b, par):
                after(pe, s_ln[5], b + 1)
                after(pe, s["maskT"], b)
                turned(pE, x2).then_inc(s["x2t_mm"], 1)

            def lg(b, par):
                after(pe, s["x2Tl"], b + 1)
                for c in range(TC):
                    mm = product(pE[:, NBLK * c:NBLK * c + NBLK],
                                 [(x2T[:, k, cols(c)], rw_sb[:, k, :]) for k in range(KC)])
                mm.then_inc(s["lg_mm"], 1)

            def mt(b, par):
                after(pe, s["nmask"], b + 1)
                for c in range(TC):
                    mm = pe.transpose(pE[0:NBLK, cols(c, 64)].bitcast(BF16), nmask[:, c, :], ident_bf[:, :])
                mm.then_inc(s["mt_mm"], 1)

            def hidden(f):
                def step(b, par):
                    after(pe, s["maskT"], b + 1)
                    after(pe, s["x2Tl"], b + 1)
                    if f == 0:
                        after(pe, s["ysum"], b)
                    elif f == 1:
                        after(pe, s_hlo[3], b)
                    else:
                        after(pe, s_hlo[f - 2], b + 1)
                    for n in range(2):
                        c = 2 * f + n
                        terms = [(expand[:, c, :], maskT[par][:, :])]
                        for k in range(KC):
                            terms += split(w1_hi[:, k, cols(c)], w1_lo[:, k, cols(c)],
                                           x2T_hi[par][:, k, :], x2T_lo[par][:, k, :])
                        mm = product(pH[f % 2][:, cols(n, S)], terms)
                    mm.then_inc(s_hmm[f], 1)
                return step

            def output(c):
                def step(b, par):
                    after(pe, s_hlo[2], b + 1)
                    terms = []
                    for k in range(FC):
                        terms += split(hid_hi[:, k, cols(c)], hid_lo[:, k, cols(c)], w2_hi[:, k, :], w2_lo[:, k, :])
                    for n, (lhs, rhs) in enumerate(terms):
                        if n == 18 and c == 0:
                            after(pe, s_hlo[3], b + 1)
                        mm = pe.matmul(pH[0][:, cols(c, E)], lhs, rhs, start=(n == 0), stop=(n == len(terms) - 1))
                    if c == TC - 1:
                        mm.then_inc(s["y_mm"], 1)
                return step

            run(pe, dict(qkv=qkv, sc=sc, ret=ret_, out1=out1, ctx=ctx_, x1t=x1t, g=g, v=v, s=s_, pt=pt, pv=pv, zt=zt,
                         cs=cs, cpt=cpt, cpv=cpv, z3t=z3t, w1=w1, x2t=x2t, lg=lg, mt=mt,
                         h0=hidden(0), h1=hidden(1), h2=hidden(2), h3=hidden(3), y0=output(0), y1=output(1)))

        def flat(t):
            return t[:, :, :].rearrange("p a b -> p (a b)")

        @block.scalar
        def _(act):
            done = s_c["act"]
            act.wait_ge(s_c["pe"], 1)
            act.activation(flat(qkv_w), pA[:, 0:384], ACT.Copy).then_inc(done, 1)
            act.activation(o_wT[:, :], pB[0:CH, 0:E], ACT.Copy, scale=scal[0:CH, 1:2]).then_inc(done, 1)
            act.wait_ge(s_c["pe"], 2)
            act.activation(flat(M_hi), pC[:, :], ACT.Copy, scale=SCALE).then_inc(done, 1)
            act.wait_ge(s_c["pe"], 3)
            act.activation(flat(McT), pD[:, :], ACT.Copy, scale=SCALE).then_inc(done, 1)
            act.activation(flat(w1_hi), flat(big1), ACT.Copy).then_inc(done, 1)
            act.wait_ge(s_ld2, 32)
            act.activation(flat(Wv_hi), flat(raw["a"]), ACT.Copy).then_inc(done, 1)
            for k in range(KC):
                act.activation(W1_hi[:, k, :], raw["b"][:, k, :], ACT.Copy, scale=g_col[:, k:k + 1]).then_inc(done, 1)
            act.wait_ge(s_ld3, 16)
            act.wait_ge(done, 5)
            act.activation(flat(w2_hi), flat(big1), ACT.Copy).then_inc(done, 1)
            act.activation(flat(z4), pC[:, :], ACT.Copy, scale=SCALE).then_inc(done, 1)

            def copy(dst, src, after_sem, n, done_sem):
                after(act, after_sem, n)
                act.activation(dst, src, ACT.Copy).then_inc(done_sem, 1)

            def qkv(b, par):
                copy(qT[:, :], pA[0:CH, 0:S], s["qkv_mm"], b + 1, s["q"])
                act.activation(kT[:, :], pA[CH:2 * CH, 0:S], ACT.Copy).then_inc(s["k"], 1)
                act.activation(flat(v_sb), pA[:, S:S + TC * CH], ACT.Copy).then_inc(s["v"], 1)

            def ret_(b, par):
                copy(ret[:, :], pA[0:CH, 0:S], s["ret_mm"], b + 1, s["ret"])

            def ctx_(b, par):
                after(act, s["cpv_mm"], b - 1)
                copy(flat(N_sb[par]), pV[:, 0:KC * SC], s["ctx_mm"], b + 1, s["N"])
                act.activation(Vc[par][0:SC, :], pV[0:SC, 256:512], ACT.Copy).then_inc(s["Vc"], 1)

            def x1t(b, par):
                copy(flat(x1T_hi), pB[:, :], s["x1t_mm"], b + 1, s["x1Th"])
                after(act, s["x1Tl"], b + 1)
                act.activation(flat(x1T), pB[:, :], ACT.Copy).then_inc(s["x1T"], 1)

            def g(b, par):
                copy(flat(G), pB[:, :], s["g_mm"], b + 1, s["G"])

            def v(b, par):
                copy(flat(V), pV[:, :], s["v_mm"], b + 1, s["V"])

            def softmax(b, blocks, bank_t, out_ap, neg, sums, s_max, s_sum):
                after(act, s_max, b + 1)
                for c, (lo, hi) in enumerate(blocks):
                    e = act.activation(out_ap(c), bank_t[:, lo:hi], ACT.Exp, bias=neg[:, c:c + 1],
                                       accum_out=sums[:, c:c + 1])
                e.then_inc(s_sum, 1)

            def s_(b, par):
                blocks = [(256, 384), (0, 256)]
                after(act, s["rsum"], b)
                softmax(b, blocks, pB, lambda c: pr[:, blocks[c][0]:blocks[c][1]], nmax, ssum, s["smax"], s["ssum"])

            def pt(b, par):
                copy(prT[:, :], pB[:, 0:384], s["pt_mm"], b + 1, s["prT"])

            def zt(b, par):
                after(act, s["zt_mm"], b + 1)
                for k in range(KC):
                    a = act.activation(hT[:, k, :], pC[:, S * k:S * k + S], ACT.Identity,
                                       scale=g_col[:, k:k + 1], bias=be_col[:, k:k + 1])
                a.then_inc(s["hT"], 1)

            def cs(b, par):
                after(act, s["rsumc"], b)
                softmax(b, [(SC * c, SC * c + SC) for c in range(TC)], pC, lambda c: prc[:, c, :], nmaxc, ssumc,
                        s["cmax"], s["csm"])

            def cpt(b, par):
                copy(prcT[0:SC, :], pC[0:SC, 0:S], s["cpt_mm"], b + 1, s["prcT"])

            def z3t(b, par):
                copy(flat(z3T_hi), pD[:, :], s["z3t_mm"], b + 1, s["z3h"])

            def x2t(b, par):
                after(act, s_hmm[3], b - 1)
                copy(flat(x2T), pE[:, :], s["x2t_mm"], b + 1, s["x2T"])
                act.activation(flat(x2T_hi[par]), pE[:, :], ACT.Copy).then_inc(s["x2Th"], 1)

            def lg(b, par):
                after(act, s["lmax"], b + 1)
                after(act, s["struck"], b)
                for c in range(TC):
                    a = act.activation(prob[:, c, 0:NBLK], logit[:, c, :], ACT.Exp, bias=lmax[:, c:c + 1])
                a.then_inc(s["prob"], 1)

            def mt(b, par):
                after(act, s_hmm[3], b - 1)
                copy(maskT[par][0:NBLK, :], pE[0:NBLK, 0:P].bitcast(BF16), s["mt_mm"], b + 1, s["maskT"])

            def hidden(f):
                def step(b, par):
                    after(act, s["y_mm"], b)
                    after(act, s_hmm[f], b + 1)
                    act.activation(hid_hi[:, 2 * f:2 * f + 2, :].rearrange("p a b -> p (a b)"), pH[f % 2][:, :],
                                   ACT.Relu).then_inc(s_hhi[f], 1)
                return step

            run(act, dict(qkv=qkv, ret=ret_, ctx=ctx_, x1t=x1t, g=g, v=v, s=s_, pt=pt, zt=zt, cs=cs, cpt=cpt, z3t=z3t,
                          x2t=x2t, lg=lg, mt=mt, h0=hidden(0), h1=hidden(1), h2=hidden(2), h3=hidden(3)))

        @block.vector
        def _(dve):
            done = s_c["dve"]
            dve.wait_ge(s_ld, N_LD)
            for k in range(KC):
                t = dve.tensor_scalar(be_wide[:, k, :], g_row[:, 0, 0:P], 0.0, be_col[:, k:k + 1], ALU.mult, ALU.add)
            t.then_inc(done, 1)
            dve.wait_ge(s_c["act"], 5)
            dve.tensor_tensor(flat(w1_lo), flat(big1), flat(w1_hi).bitcast(F32), ALU.subtract).then_inc(done, 1)
            dve.tensor_copy(b1_parts[:, 0, :], b1_rest[:, 0, :]).then_inc(s_chain, 1)
            dve.wait_ge(s_chain, 1)
            dve.tensor_tensor(b1_rest[:, 1, :], b1_rest[:, 0, :], b1_parts[:, 0, :], ALU.subtract).then_inc(done, 1)
            dve.wait_ge(done, 3)
            dve.tensor_copy(b1_parts[:, 1, :], b1_rest[:, 1, :]).then_inc(done, 1)
            dve.wait_ge(done, 4)
            dve.tensor_tensor(b1_parts[:, 2, :], b1_rest[:, 1, :], b1_parts[:, 1, :], ALU.subtract).then_inc(done, 1)
            dve.wait_ge(s_c["pool"], 21)
            dve.tensor_scalar(scal[:, 5:6], scal[:, 4:5], 1.0, None, ALU.add).then_inc(s_chain, 1)
            dve.wait_ge(s_chain, 2)
            dve.reciprocal(scal[:, 6:7], scal[:, 5:6]).then_inc(s_chain, 1)
            dve.tensor_scalar(flat(fsum)[:, 0:384], flat(x2)[:, 0:384], 0.0, None, ALU.max).then_inc(s_chain, 1)
            dve.wait_ge(s_chain, 4)
            dve.tensor_scalar(flat(fpre)[:, 0:384], flat(fsum)[:, 0:384], 0.0, scal[:, 6:7], ALU.mult, ALU.add)\
                .then_inc(done, 1)
            dve.wait_ge(s_c["act"], 8)
            dve.tensor_tensor(flat(Wv_lo), flat(raw["a"]), flat(Wv_hi).bitcast(F32), ALU.subtract).then_inc(done, 1)
            for k in range(KC):
                t = dve.scalar_tensor_tensor(W1_lo[:, k, :], raw["b"][:, k, :], g_col[:, k:k + 1],
                                             W1_hi[:, k, :].bitcast(F32), ALU.mult, ALU.subtract)
            dve.wait_ge(s_c["pe"], 4)
            for c in range(TC):
                t = dve.tensor_tensor(b1_row[:, c, :], pE[:, 0:E], b1_row[:, c, :], ALU.add)
            t.then_inc(done, 1)
            dve.wait_ge(s_c["act"], 10)
            dve.tensor_tensor(flat(w2_lo), flat(big1), flat(w2_hi).bitcast(F32), ALU.subtract).then_inc(done, 1)
            dve.tensor_tensor(flat(M_lo), flat(z4), flat(M_hi).bitcast(F32), ALU.subtract).then_inc(done, 1)
            dve.wait_ge(s_c["pool"], 24)

            def rest(lo, bank_t, hi, s_hi, b, s_lo):
                after(dve, s_hi, b + 1)
                dve.tensor_tensor(flat(lo), bank_t[:, :], flat(hi).bitcast(F32), ALU.subtract).then_inc(s_lo, 1)

            def stats(k, src, s_src, b):
                after(dve, s_src, b + 1)
                for c in range(TC):
                    t = dve.bn_stats(st[k][:, c, :], src[:, c, :])
                t.then_inc(s_stat[k], 1)
                after_apart(dve, s_stat[k], b + 1, done)
                for c in range(TC):
                    t = dve.bn_aggr(mv[k][:, c, :], st[k][:, c, :])
                t.then_inc(s_mv[k], 1)

            def normed(k, dst, src, b):
                after(dve, s_rstd[k], b + 1)
                for c in range(TC):
                    t = dve.tensor_scalar(dst[:, c, :], src[:, c, :], mv[k][:, c, 0:1], rstd[k][:, c:c + 1],
                                          ALU.subtract, ALU.mult)
                t.then_inc(s_ln[k], 1)

            def sc(b, par):
                after(dve, s["sc_mm"], b + 1)
                dve.tensor_tensor(dsc[:, :], pA[:, 0:384], dmask[:, :], ALU.mult).then_inc(s["dsc"], 1)

            def out1(b, par):
                dve.wait_ge(s_x[par], loads(b, par))
                after(dve, s["out1_mm"], b + 1)
                dve.tensor_tensor(flat(x1p), pA[:, :], flat(x_sb[par]), ALU.add).then_inc(s["x1p"], 1)
                stats(1, x1p, s["x1p"], b)

            def ln1(b, par):
                after(dve, s["x1c"], b - 1)
                after(dve, s["asum"], b - 1)
                normed(1, x1[par], x1p, b)

            def x1t(b, par):
                rest(x1T_lo, pB, x1T_hi, s["x1Th"], b, s["x1Tl"])

            def s_(b, par):
                after(dve, s["s_mm"], b + 1)
                dve.tensor_reduce(nmax[:, 0:1], pB[:, 256:384], AX.X, ALU.max, negate=True)
                dve.tensor_reduce(nmax[:, 1:2], pB[:, 0:256], AX.X, ALU.max, negate=True).then_inc(s["smax"], 1)

            def pv(b, par):
                after(dve, s["ssum"], b + 1)
                dve.reciprocal(rsum[:, :], ssum[:, :]).then_inc(s["rsum"], 1)
                after(dve, s["rsum"], b + 1)
                after(dve, s["pv_mm"], b + 1)
                for c in range(TC):
                    t = dve.scalar_tensor_tensor(asum[:, c, :], pB[:, E * c:E * c + E], rsum[:, c:c + 1],
                                                 x1[par][:, c, :], ALU.mult, ALU.add)
                t.then_inc(s["asum"], 1)
                stats(2, asum, s["asum"], b)

            def ln2(b, par):
                after(dve, s["zt_mm"], b)
                after(dve, s["h"], b)
                normed(2, z2, asum, b)

            def cs(b, par):
                after(dve, s["cs_mm"], b + 1)
                dve.tensor_reduce(nmaxc[:, :], pC[:, 0:TC * SC].rearrange("p (t k) -> p t k", t=TC), AX.X, ALU.max,
                                  negate=True).then_inc(s["cmax"], 1)

            def cpv(b, par):
                after(dve, s["csm"], b + 1)
                dve.reciprocal(rsumc[:, :], ssumc[:, :]).then_inc(s["rsumc"], 1)
                after(dve, s["rsumc"], b + 1)
                after(dve, s["cpv_mm"], b + 1)
                after(dve, s["h"], b + 1)
                for c in range(TC):
                    t = dve.scalar_tensor_tensor(csum[:, c, :], pC[:, E * c:E * c + E], rsumc[:, c:c + 1],
                                                 h[par][:, c, :], ALU.mult, ALU.add)
                t.then_inc(s["csum"], 1)
                stats(3, csum, s["csum"], b)

            def ln3(b, par):
                after(dve, s["z3t_mm"], b)
                after(dve, s["h2"], b)
                normed(3, z3, csum, b)

            def z3t(b, par):
                rest(z3T_lo, pD, z3T_hi, s["z3h"], b, s["z3l"])

            def w1(b, par):
                after(dve, s["w1_mm"], b + 1)
                dve.tensor_tensor(flat(fpre), pD[:, :], flat(b1_row), ALU.add).then_inc(s["fpre"], 1)
                after(dve, s["fpre"], b + 1)
                after(dve, s["h2"], b + 1)
                dve.scalar_tensor_tensor(flat(fsum), flat(fpre), 0.0, flat(h2[par]), ALU.max, ALU.add)\
                    .then_inc(s["fsum"], 1)
                stats(4, fsum, s["fsum"], b)

            def ln4(b, par):
                after(dve, s["z4b"], b)
                normed(4, z4, fsum, b)

            def x2sum(b, par):
                after(dve, s["z4b"], b + 1)
                after(dve, s["x1c"], b + 1)
                dve.scalar_tensor_tensor(flat(x2p), flat(z4b), 0.0, flat(x1c[par]), ALU.max, ALU.add)\
                    .then_inc(s["x2p"], 1)
                stats(5, x2p, s["x2p"], b)

            def ln5(b, par):
                after(dve, s["x2t_mm"], b)
                after(dve, s["x2b"], b)
                normed(5, x2, x2p, b)

            def x2t(b, par):
                rest(x2T_lo[par], pE, x2T_hi[par], s["x2Th"], b, s["x2Tl"])

            def lg(b, par):
                after(dve, s["lg_mm"], b + 1)
                after(dve, s["prob"], b)
                dve.tensor_tensor(flat(logit), pE[:, 0:TC * NBLK], flat(rb_row), ALU.add).then_inc(s["logit"], 1)
                after(dve, s["logit"], b + 1)
                dve.tensor_reduce(lmax[:, :], logit[:, :, :], AX.X, ALU.max, negate=True).then_inc(s["lmax"], 1)

            def mt(b, par):
                after_apart(dve, s["prob"], b + 1, done)
                for c in range(TC):
                    t = dve.max(top8[:, c, :], prob[:, c, 0:NBLK])
                t.then_inc(s["top8"], 1)
                after(dve, s["top8"], b + 1)
                dve.tensor_copy(top4[:, :, 0:TOPK], top8[:, :, 0:TOPK]).then_inc(s["top4"], 1)
                after_apart(dve, s["top4"], b + 1, done)
                for c in range(TC):
                    t = dve.match_replace(struck[:, c, :], top4[:, c, :], prob[:, c, :], -2.0)
                t.then_inc(s["struck"], 1)
                after(dve, s["struck"], b + 1)
                dve.tensor_scalar(nmask[:, :, :], struck[:, :, 0:NBLK], -1.5, -BIG, ALU.is_gt, ALU.mult)\
                    .then_inc(s["nmask"], 1)

            def hidden(f):
                def step(b, par):
                    after(dve, s_hhi[f], b + 1)
                    pair = slice(2 * f, 2 * f + 2)
                    dve.scalar_tensor_tensor(hid_lo[:, pair, :].rearrange("p a b -> p (a b)"), pH[f % 2][:, :], 0.0,
                                             hid_hi[:, pair, :].rearrange("p a b -> p (a b)").bitcast(F32),
                                             ALU.max, ALU.subtract).then_inc(s_hlo[f], 1)
                return step

            def y(b, par):
                after(dve, s["y_mm"], b + 1)
                after(dve, s["x2b"], b + 1)
                dve.tensor_tensor(flat(ysum), pH[0][:, :], flat(x2b[par]), ALU.add).then_inc(s["ysum"], 1)
                stats(6, ysum, s["ysum"], b)

            def ln6(b, par):
                if not isinstance(b, int) or b >= 2:
                    dve.wait_ge(s_st[par], loads(b, par) - 16)
                normed(6, o_sb[par], ysum, b)

            run(dve, dict(sc=sc, out1=out1, ln1=ln1, x1t=x1t, s=s_, pv=pv, ln2=ln2, cs=cs, cpv=cpv, ln3=ln3, z3t=z3t,
                          w1=w1, ln4=ln4, x2sum=x2sum, ln5=ln5, x2t=x2t, lg=lg, mt=mt,
                          h0=hidden(0), h1=hidden(1), h2=hidden(2), h3=hidden(3), y1=y, ln6=ln6))


def kernel(x, ctx_1024, L0_attn_basis, L0_attn_q_coeffs, L0_attn_k_coeffs, L0_attn_v_coeffs, L0_attn_o_coeffs,
           L0_attn_decay_logit, L0_attn_out_scale, L0_xattn_Wq, L0_xattn_Wk, L0_xattn_Wv, L0_xattn_Wcq, L0_xattn_Wck,
           L0_xattn_Wcv, L0_xattn_gamma, L0_xattn_beta, L0_xattn_W1, L0_xattn_b1, L0_ffn_router_w, L0_ffn_router_b,
           L0_ffn_w1, L0_ffn_b1, L0_ffn_w2, L0_ffn_b2):
    import numpy as np
    import concourse.bacc as bacc
    from concourse.bass_utils import run_bass_kernel_spmd

    def turn(a):
        return np.ascontiguousarray(np.swapaxes(np.asarray(a), -1, -2))

    def flat(a):
        return np.ascontiguousarray(np.asarray(a).reshape(-1))

    def columns(a):
        return np.ascontiguousarray(np.asarray(a).reshape(-1, P).T)

    laid = {
        "x": np.ascontiguousarray(x), "xT": turn(x), "ctxT": turn(ctx_1024), "basisT": turn(L0_attn_basis),
        "qcT": turn(L0_attn_q_coeffs), "kcT": turn(L0_attn_k_coeffs), "vcT": turn(L0_attn_v_coeffs),
        "ocT": turn(L0_attn_o_coeffs), "decay_logit": flat(L0_attn_decay_logit), "out_scale": flat(L0_attn_out_scale),
        "WqT": turn(L0_xattn_Wq), "WkT": turn(L0_xattn_Wk), "Wv": np.ascontiguousarray(L0_xattn_Wv),
        "WcqT": turn(L0_xattn_Wcq), "WckT": turn(L0_xattn_Wck), "Wcv": np.ascontiguousarray(L0_xattn_Wcv),
        "gamma": flat(L0_xattn_gamma), "beta": flat(L0_xattn_beta),
        "gammaC": columns(L0_xattn_gamma), "betaC": columns(L0_xattn_beta), "W1": np.ascontiguousarray(L0_xattn_W1),
        "b1": flat(L0_xattn_b1), "rwT": turn(L0_ffn_router_w), "rb": flat(L0_ffn_router_b), "w1T": turn(L0_ffn_w1),
        "fb1": flat(L0_ffn_b1), "w2T": turn(L0_ffn_w2), "fb2": flat(L0_ffn_b2),
    }
    nc = bacc.Bacc("TRN2", target_bir_lowering=False, num_devices=1)
    arrays, args = {}, []
    for name, a in laid.items():
        arrays[f"in_{name}"] = a
        args.append(nc.dram_tensor(f"in_{name}", a.shape, mybir.dt.from_np(a.dtype), kind="ExternalInput").ap())
    out = nc.dram_tensor("out_0", x.shape, mybir.dt.from_np(np.dtype(np.float32)), kind="ExternalOutput").ap()
    decoder_kernel(nc, *args, out)
    r = run_bass_kernel_spmd(nc, [arrays], core_ids=[0])
    return r.results[0]["out_0"]
```

```python
from contextlib import ExitStack

import concourse.bass as bass
from concourse import mybir

ALU = mybir.AluOpType
ACT = mybir.ActivationFunctionType
AX = mybir.AxisListType
F32 = mybir.dt.float32
F32R = mybir.dt.float32r
BF16 = mybir.dt.bfloat16

P = 128
BIG = 1e30
EPS_BLOCK = 1e-5
EPS_XATTN = 1e-3

TURN = {
    "tensor": [
        ("s", 2), ("mt", 5), ("h0", 5), ("cpt", 3), ("v", 2), ("cpv", 3), ("pt", 2), ("h1", 5),
        ("pv", 2), ("h2", 5), ("qkv", 0), ("x2t", 4), ("z3t", 3), ("h3", 5), ("ctx", 1), ("lg", 4),
        ("w1", 3), ("x1t", 1), ("sc", 0), ("y0", 5), ("zt", 2), ("ret", 0), ("g", 1), ("y1", 5),
        ("cs", 2), ("out1", 0),
    ],
    "scalar": [
        ("pt", 2), ("h1", 5), ("x2t", 4), ("z3t", 3), ("qkv", 0), ("h2", 5), ("h3", 5), ("lg", 4),
        ("x1t", 1), ("zt", 2), ("ret", 0), ("g", 1), ("ctx", 1), ("mt", 4), ("cs", 2), ("h0", 4),
        ("cpt", 2), ("s", 1), ("v", 1),
    ],
    "vector": [
        ("ln2", 2), ("h3", 5), ("sc", 0), ("x1t", 1), ("w1", 3), ("ln4", 3), ("tk", 4), ("y1", 5),
        ("cs", 2), ("out1", 0), ("s", 1), ("x2sum", 3), ("h0", 4), ("cpv", 2), ("ln5", 3),
        ("h1", 4), ("ln3", 2), ("pv", 1), ("x2t", 3), ("z3t", 2), ("h2", 4), ("ln1", 0), ("ln6", 5),
        ("lg", 3),
    ],
    "gpsimd": [
        ("ln4", 3), ("ln5", 4), ("x2sum", 3), ("out1", 0), ("cpv", 2), ("y1", 5), ("ln3", 2),
        ("pv", 1), ("ln2", 1), ("w1", 2),
    ],
}


def decoder_kernel(nc, x, xT, ctxT, basisT, qcT, kcT, vcT, ocT, decay_logit, out_scale,
                   WqT, WkT, Wv, WcqT, WckT, Wcv, gamma, beta, gammaC, betaC, W1, b1, rwT, rb, w1T, fb1, w2T, fb2, out):
    NB, S, E = x.shape
    SC = ctxT.shape[2]
    KC = E // P
    TC = S // P
    CH = qcT.shape[1]
    FF = w1T.shape[1]
    FC = FF // P
    NBLK = rwT.shape[1]
    BLK = FF // NBLK
    TOPK = NBLK // 4
    assert S == 256 and E == 256 and FC == 8
    SCALE = float(E) ** -0.5
    LAG = max(lag for steps in TURN.values() for _, lag in steps)
    SENT = 4
    NE = NBLK + SENT

    ctx = ExitStack()
    with ctx:
        def sb(name, shape, dt=F32):
            return ctx.enter_context(nc.sbuf_tensor(name, shape, dt))

        def sem(name):
            return ctx.enter_context(nc.semaphore(name))

        def bank(name):
            return ctx.enter_context(nc.psum_tensor(name, [P, 512], F32))

        pA, pB, pV, pC, pD, pE = (bank(n) for n in ("pA", "pB", "pV", "pC", "pD", "pE"))
        pH = [bank("pH0"), bank("pH1")]

        ident = sb("ident", [P, P])
        ident_bf = sb("ident_bf", [P, P], BF16)
        causal_bf = sb("causal_bf", [P, P], BF16)
        dmask = sb("dmask", [P, 384])
        qkv_w = sb("qkv_w", [P, KC, 3 * CH])
        o_wT = sb("o_wT", [CH, E])
        M_hi, M_lo = sb("M_hi", [P, KC, E], F32R), sb("M_lo", [P, KC, E], F32R)
        Wv_hi, Wv_lo = sb("Wv_hi", [P, KC, E], F32R), sb("Wv_lo", [P, KC, E], F32R)
        McT = sb("McT", [P, KC, E])
        Wcv_sb = sb("Wcv_sb", [P, KC, E])
        W1_hi, W1_lo = sb("W1_hi", [P, KC, E], F32R), sb("W1_lo", [P, KC, E], F32R)
        w1_hi, w1_lo = sb("w1_hi", [P, KC, FF], F32R), sb("w1_lo", [P, KC, FF], F32R)
        w2_hi, w2_lo = sb("w2_hi", [P, FC, E], F32R), sb("w2_lo", [P, FC, E], F32R)
        rw_sb = sb("rw_sb", [P, KC, NBLK])
        rb_row = sb("rb_row", [P, TC, NBLK])
        g_row, be_row = sb("g_row", [P, TC, E]), sb("be_row", [P, TC, E])
        b1_row, b2_row = sb("b1_row", [P, TC, E]), sb("b2_row", [P, TC, E])
        g_col, be_col = sb("g_col", [P, KC]), sb("be_col", [P, KC])
        NX = NBLK + 3
        expand = sb("expand", [NX, FC, P], BF16)
        half, eps_block, eps_xattn = sb("half", [P, TC]), sb("eps_block", [P, TC]), sb("eps_xattn", [P, TC])

        work = sb("work", [P, 20, 512])

        def shared(n):
            return work[:, n, :].rearrange("p (a b) -> p a b", a=2)

        big1 = work[:, 16:20, :].rearrange("p n e -> p (n e)").rearrange("p (k f) -> p k f", k=KC)
        big2 = work[:, 10:14, :].rearrange("p (n t) e -> p n t e", t=2).rearrange("p n t e -> p (n t e)")\
            .rearrange("p (c e) -> p c e", c=FC)
        raw = {n: shared(4 + i) for i, n in enumerate("abcd")}
        raw_v, raw_1 = shared(14), shared(15)
        basis_sb, coef = shared(8), shared(9)
        scal = sb("scal", [P, 8])
        be_wide = sb("be_wide", [P, KC, P])
        b1_parts = sb("b1_parts", [1, 3, FF], BF16)
        b1_rest = sb("b1_rest", [1, 2, FF])
        powers = sb("powers", [P, 3])
        power_of = sb("power_of", [P, 3])
        decay_col = sb("decay_col", [P, 3])
        power_step = sb("power_step", [P, 3], mybir.dt.int32)
        mirror = sb("mirror", [P, 256])
        power_dram = nc.dram_tensor("power_dram", (1, 3 * P), F32, kind="Internal")

        x_sb = [sb(f"x_sb{i}", [P, TC, E]) for i in range(2)]
        xT_sb = [sb(f"xT_sb{i}", [P, KC, S]) for i in range(2)]
        ctx_sb = [sb(f"ctx_sb{i}", [P, KC, SC]) for i in range(2)]
        qT, kT = sb("qT", [CH, S]), sb("kT", [CH, S])
        v_sb = sb("v_sb", [P, TC, CH])
        dsc = sb("dsc", [P, 384])
        ret = sb("ret", [CH, S])
        x1p = shared(0)
        x1 = [sb(f"x1_{i}", [P, TC, E]) for i in range(2)]
        x1c = [shared(10 + i) for i in range(2)]
        x1T = sb("x1T", [P, KC, S])
        x1T_hi, x1T_lo = sb("x1T_hi", [P, KC, S], F32R), sb("x1T_lo", [P, KC, S], F32R)
        G = shared(1)
        V = shared(2)
        pr = sb("pr", [P, 384])
        prT = sb("prT", [P, 384])
        nmax, ssum, rsum = sb("nmax", [P, TC]), sb("ssum", [P, TC]), sb("rsum", [P, TC])
        asum = shared(3)
        z2 = shared(8)
        hg = shared(4)
        h = [sb(f"h_{i}", [P, TC, E]) for i in range(2)]
        N_sb = [sb(f"N_sb{i}", [P, KC, SC]) for i in range(2)]
        Vc = [sb(f"Vc{i}", [P, E]) for i in range(2)]
        hT = sb("hT", [P, KC, S])
        prc = sb("prc", [P, TC, SC])
        prcT = sb("prcT", [P, S])
        nmaxc, ssumc, rsumc = sb("nmaxc", [P, TC]), sb("ssumc", [P, TC]), sb("rsumc", [P, TC])
        csum = shared(5)
        z3 = shared(6)
        h2g = shared(7)
        h2 = [sb(f"h2_{i}", [P, TC, E]) for i in range(2)]
        z3T_hi, z3T_lo = sb("z3T_hi", [P, KC, S], F32R), sb("z3T_lo", [P, KC, S], F32R)
        fpre = shared(16)
        fsum = shared(17)
        z4 = sb("z4", [P, TC, E])
        z4g, z4b = sb("z4g", [P, TC, E]), shared(9)
        x2p = shared(18)
        x2 = shared(19)
        x2b = [shared(12 + i) for i in range(2)]
        x2T = sb("x2T", [P, KC, S])
        x2T_hi = [sb(f"x2T_hi{i}", [P, KC, S], F32R) for i in range(2)]
        x2T_lo = [sb(f"x2T_lo{i}", [P, KC, S], F32R) for i in range(2)]
        logit = sb("logit", [P, TC, NBLK])
        lmax = sb("lmax", [P, TC])
        prob = sb("prob", [P, TC, NE])
        top8 = sb("top8", [P, TC, 8])
        top4 = sb("top4", [P, TC, 8])
        struck = sb("struck", [P, TC, NE])
        nmask = sb("nmask", [P, TC, NBLK], BF16)
        maskT = [sb(f"maskT{i}", [NX, S], BF16) for i in range(2)]
        hid_hi, hid_lo = sb("hid_hi", [P, FC, S], F32R), sb("hid_lo", [P, FC, S], F32R)
        ysum = sb("ysum", [P, TC, E])
        o_sb = [shared(14 + i) for i in range(2)]
        LN = range(1, 7)
        st = {k: sb(f"st{k}", [P, TC, 6]) for k in LN}
        mv = {k: sb(f"mv{k}", [P, TC, 2]) for k in LN}
        ve = {k: sb(f"ve{k}", [P, TC]) for k in LN}
        rstd = {k: sb(f"rstd{k}", [P, TC]) for k in LN}

        loaded = {n: sem(f"loaded_{n}") for n in
                  ("scal", "attn", "M", "Mc", "xattn", "b1", "w1", "w2", "rows")}
        made = {n: sem(f"made_{n}") for n in
                ("ident", "expand", "fills", "neg", "raised", "eneg", "decay", "powers", "pow_dma", "dmask",
                 "attn_mm", "attn_w", "M_mm", "hi", "lo", "Mc_mm", "Mc",
                 "be_wide", "be_mm", "b1_row", "ffn_hi", "ffn_lo",
                 "bias_parts", "bias_rows")}
        s_x = [sem(f"s_x{i}") for i in range(2)]
        s_xT = [sem(f"s_xT{i}") for i in range(2)]
        s_ctx = [sem(f"s_ctx{i}") for i in range(2)]
        s_st = [sem(f"s_st{i}") for i in range(2)]
        names = ("qkv_mm v sc_mm dsc ret_mm ret out1_mm x1p "
                 "ctx_mm Vc x1t_mm x1T x1Th x1Tl g_mm G v_mm V s_mm smax ssum pt_mm prT rsum pv_mm asum hg h "
                 "zt_mm hT cs_mm cmax csm cpt_mm prcT rsumc cpv_mm csum h2g h2 x1c "
                 "z3t_mm z3h z3l w1_mm fpre fsum z4g z4b x2p x2b "
                 "x2t_mm x2Th x2Tl lg_mm logit lmax prob top8 top4 struck nmask mt_mm maskT "
                 "y_mm ysum").split()
        s = {n: sem(f"s_{n}") for n in names}
        s_hmm = [sem(f"s_h_mm{f}") for f in range(4)]
        s_hhi = [sem(f"s_hid_hi{f}") for f in range(4)]
        s_hlo = [sem(f"s_hid_lo{f}") for f in range(4)]
        s_stat = {k: sem(f"s_stat{k}") for k in LN}
        s_mv = {k: sem(f"s_mv{k}") for k in LN}
        s_ve = {k: sem(f"s_ve{k}") for k in LN}
        s_rstd = {k: sem(f"s_rstd{k}") for k in LN}
        s_ln = {k: sem(f"s_ln{k}") for k in LN}

        def after(eng, which, n):
            if not isinstance(n, int) or n > 0:
                eng.wait_ge(which, n)

        def after_apart(eng, which, n, own):
            if not isinstance(n, int):
                n = eng.snap(n)
                eng.wait_ge(own, 1)
            after(eng, which, n)

        def loads(b, par):
            return 8 * (b - par) + 16

        def run(eng, order, steps):
            def turn(i, par):
                for name, lag in order:
                    b = i - lag
                    if not isinstance(b, int) or 0 <= b < NB:
                        steps[name](b, (par + lag) % 2)
            first = LAG + 2 + LAG % 2
            for i in range(first):
                turn(i, i % 2)
            with eng.Fori(first, NB - 1, 2) as i:
                turn(i, 0)
                turn(i + 1, 1)
            for i in range(NB, NB + LAG):
                turn(i, i % 2)

        def ready(eng, b, *what):
            if isinstance(b, int) and b == 0:
                for name, n in what:
                    eng.wait_ge(made[name], n)

        block = ctx.enter_context(nc.Block())

        @block.sync
        def _(sp):
            def rows(w):
                return w.rearrange("(k p) n -> p k n", p=P)

            def fetch(dst, src, group):
                sp.dma_start(dst, src).then_inc(loaded[group], 16)

            def first_loads():
                fetch(scal[:, 0:1], decay_logit.partition_broadcast(P), "scal")
                fetch(scal[:, 1:2], out_scale.partition_broadcast(P), "scal")
                fetch(basis_sb[:, :, :], rows(basisT), "attn")
                for n, w in enumerate((qcT, kcT, vcT, ocT)):
                    fetch(coef[:, :, n * CH:(n + 1) * CH], rows(w), "attn")
                load(0, 0)
                fetch(b1_rest[:, 0, :], fb1.rearrange("(o n) -> o n", o=1), "b1")
                fetch(raw["a"][:, :, :], rows(WqT), "M")
                fetch(raw["b"][:, :, :], rows(WkT), "M")
                fetch(raw["c"][:, :, :], rows(WcqT), "Mc")
                fetch(raw["d"][:, :, :], rows(WckT), "Mc")
                fetch(Wcv_sb[:, :, :], rows(Wcv), "xattn")
                fetch(raw_v[:, :, :], rows(Wv), "xattn")
                fetch(g_col[:, :], gammaC, "xattn")
                fetch(be_col[:, :], betaC, "xattn")
                fetch(raw_1[:, :, :], rows(W1), "xattn")
                for t in range(TC):
                    fetch(g_row[:, t, :], gamma.partition_broadcast(P), "rows")
                    fetch(be_row[:, t, :], beta.partition_broadcast(P), "rows")
                    fetch(b1_row[:, t, :], b1.partition_broadcast(P), "rows")
                    fetch(b2_row[:, t, :], fb2.partition_broadcast(P), "rows")
                    fetch(rb_row[:, t, :], rb.partition_broadcast(P), "rows")
                fetch(rw_sb[:, :, :], rows(rwT), "rows")
                fetch(big1[:, :, :], rows(w1T), "w1")
                fetch(big2, rows(w2T), "w2")
                sp.wait_ge(made["powers"], 2)
                line = power_dram.ap()
                sp.dma_start(line.rearrange("o (p q) -> (o p) q", q=3), powers[:, :]).then_inc(made["pow_dma"], 16)
                sp.wait_ge(made["pow_dma"], 16)
                hankel = bass.AP(tensor=line.tensor, offset=0, ap=[[1, P], [1, 256]])
                sp.dma_start(mirror[:, :], hankel).then_inc(made["pow_dma"], 16)
                sp.wait_ge(made["bias_parts"], 3)
                sp.wait_ge(made["expand"], 3)
                for n in range(3):
                    sp.dma_start(expand[NBLK + n:NBLK + n + 1, :, :],
                                 b1_parts[:, n, :].rearrange("o (c m) -> o c m", m=P)).then_inc(made["bias_rows"], 16)

            def load(b, par):
                after(sp, s["x1p"], b - 1)
                sp.dma_start(x_sb[par][:, :, :], x[b].rearrange("(t p) e -> p t e", p=P)).then_inc(s_x[par], 16)
                after(sp, s["qkv_mm"], b - 1)
                sp.dma_start(xT_sb[par][:, :, :], xT[b].rearrange("(k p) t -> p k t", p=P)).then_inc(s_xT[par], 16)
                after(sp, s["ctx_mm"], b - 1)
                sp.dma_start(ctx_sb[par][:, :, :], ctxT[b].rearrange("(k p) t -> p k t", p=P)).then_inc(s_ctx[par], 16)

            def store(b, par):
                after(sp, s_ln[6], b + 1)
                sp.dma_start(out[b].rearrange("(t p) e -> p t e", p=P), o_sb[par][:, :, :]).then_inc(s_st[par], 16)

            first_loads()
            lag = dict(TURN["vector"])["ln6"]

            def turn(i, par):
                if not isinstance(i, int) or 0 < i < NB:
                    load(i, par)
                j = i - lag - 1
                if not isinstance(j, int) or 0 <= j < NB:
                    store(j, (par + lag + 1) % 2)

            first = LAG + 2 + LAG % 2
            for i in range(first):
                turn(i, i % 2)
            with sp.Fori(first, NB - 1, 2) as i:
                turn(i, 0)
                turn(i + 1, 1)
            for i in range(NB, NB + lag + 1):
                turn(i, i % 2)
            for par in range(2):
                sp.wait_ge(s_st[par], 16 * (NB // 2))

        @block.gpsimd
        def _(pool):
            pool.memset(scal[:, 2:3], 2.718281828459045).then_inc(made["neg"], 1)
            pool.iota(power_step[:, :], pattern=[[1, 3]], base=-P, channel_multiplier=3).then_inc(made["raised"], 1)
            pool.wait_ge(made["raised"], 1)
            pool.tensor_copy(power_of[:, :], power_step[:, :]).then_inc(made["raised"], 1)
            pool.wait_ge(loaded["scal"], 32)
            pool.tensor_scalar(scal[:, 3:4], scal[:, 0:1], -1.0, 0.0, ALU.mult, ALU.add).then_inc(made["neg"], 1)
            pool.wait_ge(made["neg"], 2)
            pool.tensor_tensor(scal[:, 4:5], scal[:, 2:3], scal[:, 3:4], ALU.pow).then_inc(made["eneg"], 1)
            pool.memset(ident[:, :], 0.0).then_inc(made["ident"], 1)
            pool.wait_ge(made["ident"], 1)
            pool.affine_select(out=ident[:, :], in_=ident[:, :], compare_op=ALU.not_equal, fill=1.0, base=0,
                               pattern=[[-1, P]], channel_multiplier=1).then_inc(made["ident"], 1)
            pool.wait_ge(made["decay"], 2)
            pool.tensor_tensor(powers[:, :], decay_col[:, :], power_of[:, :], ALU.pow).then_inc(made["powers"], 1)
            pool.wait_ge(made["powers"], 1)
            pool.affine_select(out=powers[:, :], in_=powers[:, :], compare_op=ALU.is_ge, fill=0.0, base=-P,
                               pattern=[[1, 3]], channel_multiplier=3).then_inc(made["powers"], 1)
            pool.memset(half[:, :], -0.5).then_inc(made["fills"], 1)
            pool.memset(eps_block[:, :], EPS_BLOCK).then_inc(made["fills"], 1)
            pool.memset(eps_xattn[:, :], EPS_XATTN).then_inc(made["fills"], 1)
            pool.memset(causal_bf[:, :], 0.0).then_inc(made["ident"], 1)
            pool.wait_ge(made["ident"], 3)
            pool.affine_select(out=causal_bf[:, :], in_=causal_bf[:, :], compare_op=ALU.is_ge, fill=-BIG, base=0,
                               pattern=[[-1, P]], channel_multiplier=1).then_inc(made["ident"], 1)
            pool.tensor_copy(ident_bf[:, :], ident[:, :]).then_inc(made["ident"], 1)
            ex = expand[0:NBLK, :, :]
            pool.memset(expand[:, :, :], 1.0).then_inc(made["expand"], 1)
            pool.wait_ge(made["expand"], 1)
            pool.affine_select(out=ex, in_=ex, compare_op=ALU.is_ge, fill=0.0, base=0,
                               pattern=[[P, FC], [1, P]], channel_multiplier=-BLK).then_inc(made["expand"], 1)
            pool.wait_ge(made["expand"], 2)
            pool.affine_select(out=ex, in_=ex, compare_op=ALU.is_ge, fill=0.0, base=BLK - 1,
                               pattern=[[-P, FC], [-1, P]], channel_multiplier=BLK).then_inc(made["expand"], 1)
            for par in range(2):
                pool.memset(maskT[par][:, :], 1.0).then_inc(made["fills"], 1)
            pool.memset(prob[:, :, :], -1.0).then_inc(made["fills"], 1)
            pool.memset(top4[:, :, :], -1.0).then_inc(made["fills"], 1)
            pool.wait_ge(made["fills"], 3)
            pool.wait_ge(loaded["rows"], 16 * (5 * TC + 1))
            own = made["fills"]

            def norm_scale(k, b, eps):
                after(pool, s_mv[k], b + 1)
                pool.tensor_tensor(ve[k][:, :], mv[k][:, :, 1], eps[:, :], ALU.add).then_inc(s_ve[k], 1)
                after(pool, s_ve[k], b + 1)
                pool.tensor_tensor(rstd[k][:, :], ve[k][:, :], half[:, :], ALU.pow).then_inc(s_rstd[k], 1)

            def affine(z, zg, out_t, s_g, s_b, b):
                pool.tensor_tensor(zg[:, :, :], z[:, :, :], g_row[:, :, :], ALU.mult).then_inc(s_g, 1)
                after(pool, s_g, b + 1)
                pool.tensor_tensor(out_t[:, :, :], zg[:, :, :], be_row[:, :, :], ALU.add).then_inc(s_b, 1)

            def out1(b, par):
                norm_scale(1, b, eps_block)

            def pv(b, par):
                norm_scale(2, b, eps_xattn)

            def ln2(b, par):
                after(pool, s_ln[2], b + 1)
                after(pool, s["csum"], b - 1)
                affine(z2, hg, h[par], s["hg"], s["h"], b)

            def cpv(b, par):
                norm_scale(3, b, eps_xattn)

            def ln3(b, par):
                after(pool, s_ln[3], b + 1)
                after(pool, s["fsum"], b - 1)
                affine(z3, h2g, h2[par], s["h2g"], s["h2"], b)
                ready(pool, b, ("ffn_hi", 2), ("ffn_lo", 2))
                after_apart(pool, s_ln[1], b + 1, own)
                after(pool, s["x2p"], b - 1)
                pool.tensor_scalar(x1c[par][:, :, :], x1[par][:, :, :], 1.0, 0.0, ALU.mult, ALU.add)\
                    .then_inc(s["x1c"], 1)

            def w1(b, par):
                norm_scale(4, b, eps_xattn)

            def ln4(b, par):
                after(pool, s_ln[4], b + 1)
                after(pool, s["x2p"], b)
                affine(z4, z4g, z4b, s["z4g"], s["z4b"], b)

            def x2sum(b, par):
                norm_scale(5, b, eps_block)

            def ln5(b, par):
                after(pool, s_ln[5], b + 1)
                after(pool, s["ysum"], b - 1)
                pool.tensor_tensor(x2b[par][:, :, :], x2[:, :, :], b2_row[:, :, :], ALU.add).then_inc(s["x2b"], 1)

            def y(b, par):
                norm_scale(6, b, eps_block)

            run(pool, TURN["gpsimd"], dict(out1=out1, pv=pv, ln2=ln2, cpv=cpv, ln3=ln3, w1=w1, ln4=ln4, x2sum=x2sum, ln5=ln5, y1=y))

        @block.tensor
        def _(pe):
            def product(out_ap, terms):
                for n, (lhs, rhs) in enumerate(terms):
                    mm = pe.matmul(out_ap, lhs, rhs, start=(n == 0), stop=(n == len(terms) - 1))
                return mm

            def split(lhs_hi, lhs_lo, rhs_hi, rhs_lo):
                return [(lhs_hi, rhs_hi), (lhs_hi, rhs_lo), (lhs_lo, rhs_hi)]

            def cols(c, n=P):
                return slice(c * n, (c + 1) * n)

            pe.wait_ge(loaded["attn"], 16 * 5)
            for c in range(KC):
                mm = product(pA[:, 192 * c:192 * c + 192],
                             [(basis_sb[:, k, cols(c)], coef[:, k, 0:3 * CH]) for k in range(KC)])
            mm.then_inc(made["attn_mm"], 1)
            product(pB[0:CH, 0:E], [(coef[:, k, 3 * CH:4 * CH], basis_sb[:, k, :]) for k in range(KC)])\
                .then_inc(made["attn_mm"], 1)

            def weights():
                pe.wait_ge(loaded["M"], 32)
                for c in range(KC):
                    mm = product(pC[:, cols(c, E)], [(raw["a"][:, k, cols(c)], raw["b"][:, k, :]) for k in range(KC)])
                mm.then_inc(made["M_mm"], 1)
                pe.wait_ge(loaded["Mc"], 32)
                for c in range(KC):
                    mm = product(pD[:, cols(c, E)], [(raw["d"][:, k, cols(c)], raw["c"][:, k, :]) for k in range(KC)])
                mm.then_inc(made["Mc_mm"], 1)
                pe.wait_ge(loaded["xattn"], 80)
                pe.wait_ge(made["be_wide"], 1)
                product(pE[:, 0:E], [(be_wide[:, k, :], raw_1[:, k, :]) for k in range(KC)])\
                    .then_inc(made["be_mm"], 1)

            def qkv(b, par):
                ready(pe, b, ("attn_w", 1))
                pe.wait_ge(s_xT[par], loads(b, par))
                after(pe, s["x1p"], b)
                product(pA[:, 0:S], [(qkv_w[:, k, 0:2 * CH], xT_sb[par][:, k, :]) for k in range(KC)])
                for c in range(TC):
                    mm = product(pA[:, S + CH * c:S + CH * c + CH],
                                 [(xT_sb[par][:, k, cols(c)], qkv_w[:, k, 2 * CH:3 * CH]) for k in range(KC)])
                mm.then_inc(s["qkv_mm"], 1)

            def sc(b, par):
                after(pe, s["v"], b + 1)
                product(pA[:, 0:256], [(kT[:, P:S], qT[:, :])])
                product(pA[:, 256:384], [(kT[:, 0:P], qT[:, 0:P])]).then_inc(s["sc_mm"], 1)

            def ret_(b, par):
                after(pe, s["dsc"], b + 1)
                pe.matmul(pA[0:CH, 0:S], v_sb[:, 1, :], dsc[:, 0:256], start=True, stop=False)
                pe.matmul(pA[0:CH, 0:P], v_sb[:, 0, :], dsc[:, 256:384], start=False, stop=True)\
                    .then_inc(s["ret_mm"], 1)

            def out1(b, par):
                ready(pe, b, ("attn_w", 2))
                after(pe, s["ret"], b + 1)
                for c in range(TC):
                    mm = product(pA[:, cols(c, E)], [(ret[:, cols(c)], o_wT[:, :])])
                mm.then_inc(s["out1_mm"], 1)
                if isinstance(b, int) and b == 0:
                    weights()

            def ctx_(b, par):
                ready(pe, b, ("Mc", 1))
                if isinstance(b, int) and b == 0:
                    pe.wait_ge(loaded["xattn"], 80)
                pe.wait_ge(s_ctx[par], loads(b, par))
                after(pe, s["V"], b)
                for c in range(KC):
                    product(pV[:, SC * c:SC * c + SC],
                            [(McT[:, k, cols(c)], ctx_sb[par][:, k, :]) for k in range(KC)])
                product(pV[0:SC, 256:512], [(ctx_sb[par][:, k, :], Wcv_sb[:, k, :]) for k in range(KC)])\
                    .then_inc(s["ctx_mm"], 1)

            def turned(bank_ap, src):
                for k in range(KC):
                    for c in range(TC):
                        mm = pe.transpose(bank_ap[:, S * k + P * c:S * k + P * c + P], src[:, c, cols(k)], ident[:, :])
                return mm

            def x1t(b, par):
                ready(pe, b, ("ident", 5))
                after(pe, s_ln[1], b + 1)
                after(pe, s["asum"], b)
                turned(pB, x1[par]).then_inc(s["x1t_mm"], 1)

            def g(b, par):
                ready(pe, b, ("lo", 1))
                after(pe, s["x1T"], b + 1)
                for c in range(KC):
                    terms = []
                    for k in range(KC):
                        terms += split(M_hi[:, k, cols(c)], M_lo[:, k, cols(c)], x1T_hi[:, k, :], x1T_lo[:, k, :])
                    mm = product(pB[:, cols(c, S)], terms)
                mm.then_inc(s["g_mm"], 1)

            def v(b, par):
                ready(pe, b, ("lo", 2))
                after(pe, s["x1Tl"], b + 1)
                after(pe, s["Vc"], b + 1)
                for c in range(TC):
                    terms = []
                    for k in range(KC):
                        terms += split(x1T_hi[:, k, cols(c)], x1T_lo[:, k, cols(c)], Wv_hi[:, k, :], Wv_lo[:, k, :])
                    mm = product(pV[:, cols(c, E)], terms)
                mm.then_inc(s["v_mm"], 1)

            def s_(b, par):
                after(pe, s["G"], b + 1)
                for k in range(KC):
                    pe.matmul(pB[:, 0:256], G[:, k, P:S], x1T[:, k, :], start=(k == 0), stop=False)
                pe.matmul(pB[:, P:256], ident_bf[:, :], causal_bf[:, :], start=False, stop=True)
                for k in range(KC):
                    pe.matmul(pB[:, 256:384], G[:, k, 0:P], x1T[:, k, 0:P], start=(k == 0), stop=False)
                pe.matmul(pB[:, 256:384], ident_bf[:, :], causal_bf[:, :], start=False, stop=True)\
                    .then_inc(s["s_mm"], 1)

            def pt(b, par):
                after(pe, s["ssum"], b + 1)
                for c in range(3):
                    mm = pe.transpose(pB[:, cols(c)], pr[:, cols(c)], ident[:, :])
                mm.then_inc(s["pt_mm"], 1)

            def pv(b, par):
                after(pe, s["prT"], b + 1)
                after(pe, s["V"], b + 1)
                product(pB[:, 0:256], [(prT[:, 256:384], V[:, 0, :])])
                product(pB[:, 256:512], [(prT[:, cols(c)], V[:, c, :]) for c in range(TC)]).then_inc(s["pv_mm"], 1)

            def zt(b, par):
                ready(pe, b, ("hi", 2))
                after(pe, s_ln[2], b + 1)
                after(pe, s["csum"], b)
                turned(pC, z2).then_inc(s["zt_mm"], 1)

            def cs(b, par):
                after(pe, s["hT"], b + 1)
                after(pe, s["Vc"], b + 1)
                for c in range(TC):
                    mm = product(pC[:, SC * c:SC * c + SC],
                                 [(hT[:, k, cols(c)], N_sb[par][:, k, :]) for k in range(KC)])
                mm.then_inc(s["cs_mm"], 1)

            def cpt(b, par):
                after(pe, s["csm"], b + 1)
                for c in range(TC):
                    mm = pe.transpose(pC[0:SC, cols(c)], prc[:, c, :], ident[:, :])
                mm.then_inc(s["cpt_mm"], 1)

            def cpv(b, par):
                after(pe, s["prcT"], b + 1)
                after(pe, s["Vc"], b + 1)
                for c in range(TC):
                    mm = product(pC[:, cols(c, E)], [(prcT[0:SC, cols(c)], Vc[par][0:SC, :])])
                mm.then_inc(s["cpv_mm"], 1)

            def z3t(b, par):
                ready(pe, b, ("Mc", 1))
                after(pe, s_ln[3], b + 1)
                after(pe, s["fpre"], b)
                turned(pD, z3).then_inc(s["z3t_mm"], 1)

            def w1(b, par):
                ready(pe, b, ("lo", 4))
                after(pe, s["z3l"], b + 1)
                for c in range(TC):
                    terms = []
                    for k in range(KC):
                        terms += split(z3T_hi[:, k, cols(c)], z3T_lo[:, k, cols(c)], W1_hi[:, k, :], W1_lo[:, k, :])
                    mm = product(pD[:, cols(c, E)], terms)
                mm.then_inc(s["w1_mm"], 1)

            def x2t(b, par):
                ready(pe, b, ("b1_row", 3))
                after(pe, s_ln[5], b + 1)
                after(pe, s["maskT"], b)
                turned(pE, x2).then_inc(s["x2t_mm"], 1)

            def lg(b, par):
                if isinstance(b, int) and b == 0:
                    pe.wait_ge(loaded["rows"], 16 * (5 * TC + 1))
                after(pe, s["x2Tl"], b + 1)
                for c in range(TC):
                    mm = product(pE[:, NBLK * c:NBLK * c + NBLK],
                                 [(x2T[:, k, cols(c)], rw_sb[:, k, :]) for k in range(KC)])
                mm.then_inc(s["lg_mm"], 1)

            def mt(b, par):
                after(pe, s["nmask"], b + 1)
                for c in range(TC):
                    mm = pe.transpose(pE[0:NBLK, cols(c, 64)].bitcast(BF16), nmask[:, c, :], ident_bf[:, :])
                mm.then_inc(s["mt_mm"], 1)

            def hidden(f):
                def step(b, par):
                    ready(pe, b, ("ffn_hi", 1), ("ffn_lo", 1))
                    if isinstance(b, int) and b == 0:
                        pe.wait_ge(made["bias_rows"], 48)
                    after(pe, s["x2Tl"], b + 1)
                    if f == 0:
                        after(pe, s["ysum"], b)
                    elif f == 1:
                        after(pe, s_hlo[3], b)
                    else:
                        after(pe, s_hlo[f - 2], b + 1)
                    for n in range(2):
                        c = 2 * f + n
                        terms = []
                        for k in range(KC):
                            terms += split(w1_hi[:, k, cols(c)], w1_lo[:, k, cols(c)],
                                           x2T_hi[par][:, k, :], x2T_lo[par][:, k, :])
                        for m, (lhs, rhs) in enumerate(terms):
                            pe.matmul(pH[f % 2][:, cols(n, S)], lhs, rhs, start=(m == 0), stop=False)
                        after(pe, s["maskT"], b + 1)
                        mm = pe.matmul(pH[f % 2][:, cols(n, S)], expand[:, c, :], maskT[par][:, :], start=False,
                                       stop=True)
                    mm.then_inc(s_hmm[f], 1)
                return step

            def output(c):
                def step(b, par):
                    ready(pe, b, ("ffn_hi", 2), ("ffn_lo", 2))
                    after(pe, s_hlo[2], b + 1)
                    terms = []
                    for k in range(FC):
                        terms += split(hid_hi[:, k, cols(c)], hid_lo[:, k, cols(c)], w2_hi[:, k, :], w2_lo[:, k, :])
                    for n, (lhs, rhs) in enumerate(terms):
                        if n == 18 and c == 0:
                            after(pe, s_hlo[3], b + 1)
                        mm = pe.matmul(pH[0][:, cols(c, E)], lhs, rhs, start=(n == 0), stop=(n == len(terms) - 1))
                    if c == TC - 1:
                        mm.then_inc(s["y_mm"], 1)
                return step

            run(pe, TURN["tensor"], dict(qkv=qkv, sc=sc, ret=ret_, out1=out1, ctx=ctx_, x1t=x1t, g=g, v=v, s=s_, pt=pt, pv=pv, zt=zt,
                         cs=cs, cpt=cpt, cpv=cpv, z3t=z3t, w1=w1, x2t=x2t, lg=lg, mt=mt,
                         h0=hidden(0), h1=hidden(1), h2=hidden(2), h3=hidden(3), y0=output(0), y1=output(1)))

        def flat(t):
            return t[:, :, :].rearrange("p a b -> p (a b)")

        @block.scalar
        def _(act):
            act.wait_ge(made["attn_mm"], 1)
            act.activation(flat(qkv_w), pA[:, 0:384], ACT.Copy).then_inc(made["attn_w"], 1)
            act.wait_ge(made["attn_mm"], 2)
            act.wait_ge(loaded["scal"], 32)
            act.activation(o_wT[:, :], pB[0:CH, 0:E], ACT.Copy, scale=scal[0:CH, 1:2]).then_inc(made["attn_w"], 1)

            def weights():
                act.wait_ge(made["M_mm"], 1)
                act.activation(flat(M_hi), pC[:, :], ACT.Copy, scale=SCALE).then_inc(made["hi"], 1)
                act.activation(flat(z4), pC[:, :], ACT.Copy, scale=SCALE).then_inc(made["hi"], 1)
                act.wait_ge(made["Mc_mm"], 1)
                act.activation(flat(McT), pD[:, :], ACT.Copy, scale=SCALE).then_inc(made["Mc"], 1)
                act.wait_ge(loaded["xattn"], 80)
                act.activation(flat(Wv_hi), flat(raw_v), ACT.Copy).then_inc(made["hi"], 1)
                for k in range(KC):
                    act.activation(W1_hi[:, k, :], raw_1[:, k, :], ACT.Copy, scale=g_col[:, k:k + 1])\
                        .then_inc(made["hi"], 1)

            def ffn_weights():
                act.wait_ge(loaded["w1"], 16)
                act.activation(flat(w1_hi), flat(big1), ACT.Copy).then_inc(made["ffn_hi"], 1)
                act.wait_ge(loaded["w2"], 16)
                act.activation(flat(w2_hi), flat(big2), ACT.Copy).then_inc(made["ffn_hi"], 1)

            def copy(dst, src, after_sem, n, done_sem):
                after(act, after_sem, n)
                act.activation(dst, src, ACT.Copy).then_inc(done_sem, 1)

            def qkv(b, par):
                after(act, s["qkv_mm"], b + 1)
                act.activation(qT[:, :], pA[0:CH, 0:S], ACT.Copy)
                act.activation(kT[:, :], pA[CH:2 * CH, 0:S], ACT.Copy)
                act.activation(flat(v_sb), pA[:, S:S + TC * CH], ACT.Copy).then_inc(s["v"], 1)

            def ret_(b, par):
                copy(ret[:, :], pA[0:CH, 0:S], s["ret_mm"], b + 1, s["ret"])
                if isinstance(b, int) and b == 0:
                    weights()
                    ffn_weights()

            def ctx_(b, par):
                after(act, s["cpv_mm"], b - 1)
                after(act, s["ctx_mm"], b + 1)
                act.activation(flat(N_sb[par]), pV[:, 0:KC * SC], ACT.Copy)
                act.activation(Vc[par][0:SC, :], pV[0:SC, 256:512], ACT.Copy).then_inc(s["Vc"], 1)

            def x1t(b, par):
                copy(flat(x1T_hi), pB[:, :], s["x1t_mm"], b + 1, s["x1Th"])
                after(act, s["x1Tl"], b + 1)
                act.activation(flat(x1T), pB[:, :], ACT.Copy).then_inc(s["x1T"], 1)

            def g(b, par):
                copy(flat(G), pB[:, :], s["g_mm"], b + 1, s["G"])

            def v(b, par):
                copy(flat(V), pV[:, :], s["v_mm"], b + 1, s["V"])

            def softmax(b, blocks, bank_t, out_ap, neg, sums, s_max, s_sum):
                after(act, s_max, b + 1)
                for c, (lo, hi) in enumerate(blocks):
                    e = act.activation(out_ap(c), bank_t[:, lo:hi], ACT.Exp, bias=neg[:, c:c + 1],
                                       accum_out=sums[:, c:c + 1])
                e.then_inc(s_sum, 1)

            def s_(b, par):
                blocks = [(256, 384), (0, 256)]
                after(act, s["rsum"], b)
                softmax(b, blocks, pB, lambda c: pr[:, blocks[c][0]:blocks[c][1]], nmax, ssum, s["smax"], s["ssum"])

            def pt(b, par):
                copy(prT[:, :], pB[:, 0:384], s["pt_mm"], b + 1, s["prT"])

            def zt(b, par):
                after(act, s["zt_mm"], b + 1)
                for k in range(KC):
                    a = act.activation(hT[:, k, :], pC[:, S * k:S * k + S], ACT.Identity,
                                       scale=g_col[:, k:k + 1], bias=be_col[:, k:k + 1])
                a.then_inc(s["hT"], 1)

            def cs(b, par):
                after(act, s["rsumc"], b)
                softmax(b, [(SC * c, SC * c + SC) for c in range(TC)], pC, lambda c: prc[:, c, :], nmaxc, ssumc,
                        s["cmax"], s["csm"])

            def cpt(b, par):
                copy(prcT[0:SC, :], pC[0:SC, 0:S], s["cpt_mm"], b + 1, s["prcT"])

            def z3t(b, par):
                copy(flat(z3T_hi), pD[:, :], s["z3t_mm"], b + 1, s["z3h"])

            def x2t(b, par):
                after(act, s_hmm[3], b - 1)
                after(act, s["x2t_mm"], b + 1)
                act.activation(flat(x2T), pE[:, :], ACT.Copy)
                act.activation(flat(x2T_hi[par]), pE[:, :], ACT.Copy).then_inc(s["x2Th"], 1)

            def lg(b, par):
                after(act, s["lmax"], b + 1)
                after(act, s["struck"], b)
                for c in range(TC):
                    a = act.activation(prob[:, c, 0:NBLK], logit[:, c, :], ACT.Exp, bias=lmax[:, c:c + 1])
                a.then_inc(s["prob"], 1)

            def mt(b, par):
                after(act, s_hmm[3], b - 1)
                copy(maskT[par][0:NBLK, :], pE[0:NBLK, 0:P].bitcast(BF16), s["mt_mm"], b + 1, s["maskT"])

            def hidden(f):
                def step(b, par):
                    after(act, s["y_mm"], b)
                    after(act, s_hmm[f], b + 1)
                    act.activation(hid_hi[:, 2 * f:2 * f + 2, :].rearrange("p a b -> p (a b)"), pH[f % 2][:, :],
                                   ACT.Relu).then_inc(s_hhi[f], 1)
                return step

            run(act, TURN["scalar"], dict(qkv=qkv, ret=ret_, ctx=ctx_, x1t=x1t, g=g, v=v, s=s_, pt=pt, zt=zt, cs=cs, cpt=cpt, z3t=z3t,
                          x2t=x2t, lg=lg, mt=mt, h0=hidden(0), h1=hidden(1), h2=hidden(2), h3=hidden(3)))

        @block.vector
        def _(dve):
            dve.wait_ge(made["eneg"], 1)
            dve.tensor_scalar(scal[:, 5:6], scal[:, 4:5], 1.0, None, ALU.add).then_inc(made["decay"], 1)
            dve.wait_ge(made["decay"], 1)
            dve.reciprocal(scal[:, 6:7], scal[:, 5:6]).then_inc(made["neg"], 1)
            dve.wait_ge(made["neg"], 3)
            dve.wait_ge(made["raised"], 2)
            dve.tensor_scalar(decay_col[:, :], power_of[:, :], 0.0, scal[:, 6:7], ALU.mult, ALU.add)\
                .then_inc(made["decay"], 1)
            parts = made["bias_parts"]
            dve.wait_ge(loaded["b1"], 16)
            dve.tensor_copy(b1_parts[:, 0, :], b1_rest[:, 0, :]).then_inc(parts, 1)
            dve.wait_ge(parts, 1)
            dve.tensor_tensor(b1_rest[:, 1, :], b1_rest[:, 0, :], b1_parts[:, 0, :], ALU.subtract)\
                .then_inc(made["b1_row"], 1)
            dve.wait_ge(made["b1_row"], 1)
            dve.tensor_copy(b1_parts[:, 1, :], b1_rest[:, 1, :]).then_inc(parts, 1)
            dve.wait_ge(parts, 2)
            dve.tensor_tensor(b1_parts[:, 2, :], b1_rest[:, 1, :], b1_parts[:, 1, :], ALU.subtract)\
                .then_inc(parts, 1)
            dve.wait_ge(made["pow_dma"], 32)
            dve.tensor_copy(dmask[:, 0:256], mirror[:, ::-1]).then_inc(made["dmask"], 1)
            dve.tensor_copy(dmask[:, 256:384], mirror[:, P - 1::-1]).then_inc(made["dmask"], 1)
            dve.wait_ge(made["dmask"], 2)
            own = made["dmask"]

            def weights():
                dve.wait_ge(loaded["xattn"], 80)
                dve.wait_ge(loaded["rows"], 16 * (5 * TC + 1))
                for k in range(KC):
                    t = dve.tensor_scalar(be_wide[:, k, :], g_row[:, 0, 0:P], 0.0, be_col[:, k:k + 1],
                                          ALU.mult, ALU.add)
                t.then_inc(made["be_wide"], 1)
                dve.wait_ge(made["hi"], 2)
                dve.tensor_tensor(flat(M_lo), flat(z4), flat(M_hi).bitcast(F32), ALU.subtract)\
                    .then_inc(made["lo"], 1)
                dve.wait_ge(made["hi"], 3)
                dve.tensor_tensor(flat(Wv_lo), flat(raw_v), flat(Wv_hi).bitcast(F32), ALU.subtract)\
                    .then_inc(made["lo"], 1)
                dve.wait_ge(made["hi"], 5)
                for k in range(KC):
                    dve.scalar_tensor_tensor(W1_lo[:, k, :], raw_1[:, k, :], g_col[:, k:k + 1],
                                             W1_hi[:, k, :].bitcast(F32), ALU.mult, ALU.subtract)\
                        .then_inc(made["lo"], 1)
                dve.wait_ge(made["be_mm"], 1)
                for c in range(TC):
                    dve.tensor_tensor(b1_row[:, c, :], pE[:, 0:E], b1_row[:, c, :], ALU.add)\
                        .then_inc(made["b1_row"], 1)

            def ffn_weights():
                dve.wait_ge(made["ffn_hi"], 1)
                dve.tensor_tensor(flat(w1_lo), flat(big1), flat(w1_hi).bitcast(F32), ALU.subtract)\
                    .then_inc(made["ffn_lo"], 1)
                dve.wait_ge(made["ffn_hi"], 2)
                dve.tensor_tensor(flat(w2_lo), flat(big2), flat(w2_hi).bitcast(F32), ALU.subtract)\
                    .then_inc(made["ffn_lo"], 1)

            def rest(lo, bank_t, hi, s_hi, b, s_lo):
                after(dve, s_hi, b + 1)
                dve.tensor_tensor(flat(lo), bank_t[:, :], flat(hi).bitcast(F32), ALU.subtract).then_inc(s_lo, 1)

            def stats(k, src, s_src, b):
                after(dve, s_src, b + 1)
                for c in range(TC):
                    t = dve.bn_stats(st[k][:, c, :], src[:, c, :])
                t.then_inc(s_stat[k], 1)
                after_apart(dve, s_stat[k], b + 1, own)
                for c in range(TC):
                    t = dve.bn_aggr(mv[k][:, c, :], st[k][:, c, :])
                t.then_inc(s_mv[k], 1)

            def normed(k, dst, src, b):
                after(dve, s_rstd[k], b + 1)
                for c in range(TC):
                    t = dve.tensor_scalar(dst[:, c, :], src[:, c, :], mv[k][:, c, 0:1], rstd[k][:, c:c + 1],
                                          ALU.subtract, ALU.mult)
                t.then_inc(s_ln[k], 1)

            def sc(b, par):
                after(dve, s["sc_mm"], b + 1)
                dve.tensor_tensor(dsc[:, :], pA[:, 0:384], dmask[:, :], ALU.mult).then_inc(s["dsc"], 1)

            def out1(b, par):
                dve.wait_ge(s_x[par], loads(b, par))
                after(dve, s["out1_mm"], b + 1)
                dve.tensor_tensor(flat(x1p), pA[:, :], flat(x_sb[par]), ALU.add).then_inc(s["x1p"], 1)
                stats(1, x1p, s["x1p"], b)

            def ln1(b, par):
                after(dve, s["x1c"], b - 1)
                after(dve, s["asum"], b - 1)
                normed(1, x1[par], x1p, b)
                if isinstance(b, int) and b == 0:
                    weights()
                    ffn_weights()

            def x1t(b, par):
                rest(x1T_lo, pB, x1T_hi, s["x1Th"], b, s["x1Tl"])

            def s_(b, par):
                after(dve, s["s_mm"], b + 1)
                dve.tensor_reduce(nmax[:, 0:1], pB[:, 256:384], AX.X, ALU.max, negate=True)
                dve.tensor_reduce(nmax[:, 1:2], pB[:, 0:256], AX.X, ALU.max, negate=True).then_inc(s["smax"], 1)

            def pv(b, par):
                after(dve, s["ssum"], b + 1)
                dve.reciprocal(rsum[:, :], ssum[:, :]).then_inc(s["rsum"], 1)
                after(dve, s["rsum"], b + 1)
                after(dve, s["pv_mm"], b + 1)
                for c in range(TC):
                    t = dve.scalar_tensor_tensor(asum[:, c, :], pB[:, E * c:E * c + E], rsum[:, c:c + 1],
                                                 x1[par][:, c, :], ALU.mult, ALU.add)
                t.then_inc(s["asum"], 1)
                stats(2, asum, s["asum"], b)

            def ln2(b, par):
                after(dve, s["zt_mm"], b)
                after(dve, s["h"], b)
                normed(2, z2, asum, b)

            def cs(b, par):
                after(dve, s["cs_mm"], b + 1)
                dve.tensor_reduce(nmaxc[:, :], pC[:, 0:TC * SC].rearrange("p (t k) -> p t k", t=TC), AX.X, ALU.max,
                                  negate=True).then_inc(s["cmax"], 1)

            def cpv(b, par):
                after(dve, s["csm"], b + 1)
                dve.reciprocal(rsumc[:, :], ssumc[:, :]).then_inc(s["rsumc"], 1)
                after(dve, s["rsumc"], b + 1)
                after(dve, s["cpv_mm"], b + 1)
                after(dve, s["h"], b + 1)
                for c in range(TC):
                    t = dve.scalar_tensor_tensor(csum[:, c, :], pC[:, E * c:E * c + E], rsumc[:, c:c + 1],
                                                 h[par][:, c, :], ALU.mult, ALU.add)
                t.then_inc(s["csum"], 1)
                stats(3, csum, s["csum"], b)

            def ln3(b, par):
                after(dve, s["z3t_mm"], b)
                after(dve, s["h2"], b)
                normed(3, z3, csum, b)

            def z3t(b, par):
                rest(z3T_lo, pD, z3T_hi, s["z3h"], b, s["z3l"])

            def w1(b, par):
                after(dve, s["w1_mm"], b + 1)
                dve.tensor_tensor(flat(fpre), pD[:, :], flat(b1_row), ALU.add).then_inc(s["fpre"], 1)
                after(dve, s["fpre"], b + 1)
                after(dve, s["h2"], b + 1)
                dve.scalar_tensor_tensor(flat(fsum), flat(fpre), 0.0, flat(h2[par]), ALU.max, ALU.add)\
                    .then_inc(s["fsum"], 1)
                stats(4, fsum, s["fsum"], b)

            def ln4(b, par):
                after(dve, s["z4b"], b)
                normed(4, z4, fsum, b)

            def x2sum(b, par):
                after(dve, s["z4b"], b + 1)
                after(dve, s["x1c"], b + 1)
                dve.scalar_tensor_tensor(flat(x2p), flat(z4b), 0.0, flat(x1c[par]), ALU.max, ALU.add)\
                    .then_inc(s["x2p"], 1)
                stats(5, x2p, s["x2p"], b)

            def ln5(b, par):
                after(dve, s["x2t_mm"], b)
                after(dve, s["x2b"], b)
                normed(5, x2, x2p, b)

            def x2t(b, par):
                rest(x2T_lo[par], pE, x2T_hi[par], s["x2Th"], b, s["x2Tl"])

            def lg(b, par):
                after(dve, s["lg_mm"], b + 1)
                after(dve, s["prob"], b)
                dve.tensor_tensor(flat(logit), pE[:, 0:TC * NBLK], flat(rb_row), ALU.add).then_inc(s["logit"], 1)
                after(dve, s["logit"], b + 1)
                dve.tensor_reduce(lmax[:, :], logit[:, :, :], AX.X, ALU.max, negate=True).then_inc(s["lmax"], 1)

            def tk(b, par):
                after_apart(dve, s["prob"], b + 1, own)
                for c in range(TC):
                    t = dve.max(top8[:, c, :], prob[:, c, 0:NBLK])
                t.then_inc(s["top8"], 1)
                after(dve, s["top8"], b + 1)
                dve.tensor_copy(top4[:, :, 0:TOPK], top8[:, :, 0:TOPK]).then_inc(s["top4"], 1)
                after_apart(dve, s["top4"], b + 1, own)
                for c in range(TC):
                    t = dve.match_replace(struck[:, c, :], top4[:, c, :], prob[:, c, :], -2.0)
                t.then_inc(s["struck"], 1)
                after(dve, s["struck"], b + 1)
                dve.tensor_scalar(nmask[:, :, :], struck[:, :, 0:NBLK], -1.5, -BIG, ALU.is_gt, ALU.mult)\
                    .then_inc(s["nmask"], 1)

            def hidden(f):
                def step(b, par):
                    after(dve, s_hhi[f], b + 1)
                    pair = slice(2 * f, 2 * f + 2)
                    dve.scalar_tensor_tensor(hid_lo[:, pair, :].rearrange("p a b -> p (a b)"), pH[f % 2][:, :], 0.0,
                                             hid_hi[:, pair, :].rearrange("p a b -> p (a b)").bitcast(F32),
                                             ALU.max, ALU.subtract).then_inc(s_hlo[f], 1)
                return step

            def y(b, par):
                after(dve, s["y_mm"], b + 1)
                after(dve, s["x2b"], b + 1)
                dve.tensor_tensor(flat(ysum), pH[0][:, :], flat(x2b[par]), ALU.add).then_inc(s["ysum"], 1)
                stats(6, ysum, s["ysum"], b)

            def ln6(b, par):
                if not isinstance(b, int) or b >= 2:
                    dve.wait_ge(s_st[par], loads(b, par) - 16)
                normed(6, o_sb[par], ysum, b)

            run(dve, TURN["vector"], dict(sc=sc, out1=out1, ln1=ln1, x1t=x1t, s=s_, pv=pv, ln2=ln2, cs=cs, cpv=cpv, ln3=ln3, z3t=z3t,
                          w1=w1, ln4=ln4, x2sum=x2sum, ln5=ln5, x2t=x2t, lg=lg, tk=tk,
                          h0=hidden(0), h1=hidden(1), h2=hidden(2), h3=hidden(3), y1=y, ln6=ln6))


def kernel(x, ctx_1024, L0_attn_basis, L0_attn_q_coeffs, L0_attn_k_coeffs, L0_attn_v_coeffs, L0_attn_o_coeffs,
           L0_attn_decay_logit, L0_attn_out_scale, L0_xattn_Wq, L0_xattn_Wk, L0_xattn_Wv, L0_xattn_Wcq, L0_xattn_Wck,
           L0_xattn_Wcv, L0_xattn_gamma, L0_xattn_beta, L0_xattn_W1, L0_xattn_b1, L0_ffn_router_w, L0_ffn_router_b,
           L0_ffn_w1, L0_ffn_b1, L0_ffn_w2, L0_ffn_b2):
    import numpy as np
    import concourse.bacc as bacc
    from concourse.bass_utils import run_bass_kernel_spmd

    def turn(a):
        return np.ascontiguousarray(np.swapaxes(np.asarray(a), -1, -2))

    def flat(a):
        return np.ascontiguousarray(np.asarray(a).reshape(-1))

    def columns(a):
        return np.ascontiguousarray(np.asarray(a).reshape(-1, P).T)

    laid = {
        "x": np.ascontiguousarray(x), "xT": turn(x), "ctxT": turn(ctx_1024), "basisT": turn(L0_attn_basis),
        "qcT": turn(L0_attn_q_coeffs), "kcT": turn(L0_attn_k_coeffs), "vcT": turn(L0_attn_v_coeffs),
        "ocT": turn(L0_attn_o_coeffs), "decay_logit": flat(L0_attn_decay_logit), "out_scale": flat(L0_attn_out_scale),
        "WqT": turn(L0_xattn_Wq), "WkT": turn(L0_xattn_Wk), "Wv": np.ascontiguousarray(L0_xattn_Wv),
        "WcqT": turn(L0_xattn_Wcq), "WckT": turn(L0_xattn_Wck), "Wcv": np.ascontiguousarray(L0_xattn_Wcv),
        "gamma": flat(L0_xattn_gamma), "beta": flat(L0_xattn_beta),
        "gammaC": columns(L0_xattn_gamma), "betaC": columns(L0_xattn_beta), "W1": np.ascontiguousarray(L0_xattn_W1),
        "b1": flat(L0_xattn_b1), "rwT": turn(L0_ffn_router_w), "rb": flat(L0_ffn_router_b), "w1T": turn(L0_ffn_w1),
        "fb1": flat(L0_ffn_b1), "w2T": turn(L0_ffn_w2), "fb2": flat(L0_ffn_b2),
    }
    nc = bacc.Bacc("TRN2", target_bir_lowering=False, num_devices=1)
    arrays, args = {}, []
    for name, a in laid.items():
        arrays[f"in_{name}"] = a
        args.append(nc.dram_tensor(f"in_{name}", a.shape, mybir.dt.from_np(a.dtype), kind="ExternalInput").ap())
    out = nc.dram_tensor("out_0", x.shape, mybir.dt.from_np(np.dtype(np.float32)), kind="ExternalOutput").ap()
    decoder_kernel(nc, *args, out)
    r = run_bass_kernel_spmd(nc, [arrays], core_ids=[0])
    return r.results[0]["out_0"]
```

```python
from contextlib import ExitStack

import concourse.bass as bass
from concourse import mybir

ALU = mybir.AluOpType
ACT = mybir.ActivationFunctionType
AX = mybir.AxisListType
F32 = mybir.dt.float32
F32R = mybir.dt.float32r
BF16 = mybir.dt.bfloat16

P = 128
BIG = 1e30
EPS_BLOCK = 1e-5
EPS_XATTN = 1e-3

TURN = {
    "tensor": [
        ("qkv", 0), ("zt", 2), ("g", 1), ("mt", 4), ("cs", 2), ("sc", 0), ("h0", 4), ("cpt", 2),
        ("s", 1), ("cpv", 2), ("ret", 0), ("v", 1), ("h1", 4), ("pt", 1), ("h2", 4), ("out1", 0),
        ("x2t", 3), ("z3t", 2), ("pv", 1), ("h3", 4), ("ctx", 0), ("w1", 2), ("y0", 4), ("lg", 3),
        ("x1t", 0), ("y1", 4),
    ],
    "scalar": [
        ("x1t", 1), ("ctx", 1), ("lg", 4), ("zt", 2), ("qkv", 0), ("mt", 4), ("g", 1), ("cs", 2),
        ("cx", 0), ("cpt", 2), ("h0", 4), ("ret", 0), ("s", 1), ("v", 1), ("h1", 4), ("pt", 1),
        ("h2", 4), ("z3t", 2), ("x2t", 3), ("h3", 4),
    ],
    "vector": [
        ("sc", 0), ("h0", 4), ("s", 1), ("cpv", 2), ("ret", 0), ("ln5", 3), ("v", 1), ("ln3", 2),
        ("pt", 1), ("h1", 4), ("out1", 0), ("h2", 4), ("z3t", 2), ("ln6", 5), ("pv", 1), ("h3", 4),
        ("x2t", 3), ("ln1", 0), ("w1", 2), ("x1t", 0), ("ln2", 1), ("lg", 3), ("ln4", 2), ("tk", 3),
        ("ctx", 0), ("y1", 4), ("cs", 1), ("g", 0), ("x2sum", 2), ("cpt", 1),
    ],
    "gpsimd": [
        ("x2sum", 3), ("cpv", 2), ("cx", 0), ("ln3", 2), ("out1", 0), ("ln5", 3), ("pv", 1),
        ("w1", 2), ("ln4", 2), ("ln2", 1), ("y1", 4),
    ],
}


def decoder_kernel(nc, x, xT, ctxT, basisT, qcT, kcT, vcT, ocT, decay_logit, out_scale,
                   WqT, WkT, Wv, WcqT, WckT, Wcv, gamma, beta, gammaC, betaC, W1, b1, rwT, rb, w1T, fb1, w2T, fb2, out):
    NB, S, E = x.shape
    SC = ctxT.shape[2]
    KC = E // P
    TC = S // P
    CH = qcT.shape[1]
    FF = w1T.shape[1]
    FC = FF // P
    NBLK = rwT.shape[1]
    BLK = FF // NBLK
    TOPK = NBLK // 4
    assert S == 256 and E == 256 and FC == 8
    SCALE = float(E) ** -0.5
    LAG = max(lag for steps in TURN.values() for _, lag in steps)
    NE = NBLK + 8 - TOPK

    ctx = ExitStack()
    with ctx:
        def sb(name, shape, dt=F32):
            return ctx.enter_context(nc.sbuf_tensor(name, shape, dt))

        def sem(name):
            return ctx.enter_context(nc.semaphore(name))

        def bank(name):
            return ctx.enter_context(nc.psum_tensor(name, [P, 512], F32))

        pA, pB, pV, pC, pD, pE = (bank(n) for n in ("pA", "pB", "pV", "pC", "pD", "pE"))
        pH = [bank("pH0"), bank("pH1")]

        ident = sb("ident", [P, P])
        ident_bf = sb("ident_bf", [P, P], BF16)
        causal_bf = sb("causal_bf", [P, P], BF16)
        dmask = sb("dmask", [P, 384])
        qkv_w = sb("qkv_w", [P, KC, 3 * CH])
        o_wT, ow_lo = sb("o_wT", [CH, E]), sb("ow_lo", [CH, E], F32R)
        ow_hi = sb("ow_hi", [2 * CH, E], F32R)
        M_hi, M_lo = sb("M_hi", [P, KC, E], F32R), sb("M_lo", [P, KC, E], F32R)
        Wv_hi, Wv_lo = sb("Wv_hi", [P, KC, E], F32R), sb("Wv_lo", [P, KC, E], F32R)
        McT = sb("McT", [P, KC, E])
        Wcv_hi, Wcv_lo = sb("Wcv_hi", [P, KC, E], F32R), sb("Wcv_lo", [P, KC, E], F32R)
        W1_hi, W1_lo = sb("W1_hi", [P, KC, E], F32R), sb("W1_lo", [P, KC, E], F32R)
        w1_hi, w1_lo = sb("w1_hi", [P, KC, FF], F32R), sb("w1_lo", [P, KC, FF], F32R)
        w2_hi, w2_lo = sb("w2_hi", [P, FC, E], F32R), sb("w2_lo", [P, FC, E], F32R)
        rw_sb = sb("rw_sb", [P, KC, NBLK])
        rb_row = sb("rb_row", [P, TC, NBLK])
        g_row, be_row = sb("g_row", [P, TC, E]), sb("be_row", [P, TC, E])
        b1_row, b2_row = sb("b1_row", [P, TC, E]), sb("b2_row", [P, TC, E])
        g_col, be_col = sb("g_col", [P, KC]), sb("be_col", [P, KC])
        NX = NBLK + 3
        expand = sb("expand", [NX, FC, P], BF16)
        half, eps_block, eps_xattn = sb("half", [P, TC]), sb("eps_block", [P, TC]), sb("eps_xattn", [P, TC])

        work = sb("work", [P, 20, 512])

        def shared(n, t=work):
            return t[:, n, :].rearrange("p (a b) -> p a b", a=2)

        raw_w1 = work[:, 16:20, :].rearrange("p n e -> p (n e)").rearrange("p (k f) -> p k f", k=KC)
        raw_w2 = work[:, 10:14, :].rearrange("p (n t) e -> p n t e", t=2).rearrange("p n t e -> p (n t e)")\
            .rearrange("p (c e) -> p c e", c=FC)
        raw = {n: shared(4 + i) for i, n in enumerate("abcd")}
        raw_v, raw_1 = shared(14), shared(15)
        basis_sb, coef = shared(8), shared(9)
        Wcv_sb = shared(1)
        scal = sb("scal", [P, 8])
        be_wide = work[:, 2, 256:512].rearrange("p (k n) -> p k n", k=KC)
        b1_parts = sb("b1_parts", [1, 3, FF], BF16)
        late = sb("late", [P, 4, 512])
        b1_rest = late[0:1, :, :].rearrange("o n e -> o (n e)").rearrange("o (n f) -> o n f", n=2)
        powers = sb("powers", [P, 3])
        power_of = sb("power_of", [P, 3])
        decay_col = sb("decay_col", [P, 3])
        power_step = sb("power_step", [P, 3], mybir.dt.int32)
        mirror = work[:, 2, 0:256]
        power_dram = nc.dram_tensor("power_dram", (1, 3 * P), F32, kind="Internal")

        x_sb = [sb(f"x_sb{i}", [P, TC, E]) for i in range(2)]
        xT_sb = [sb(f"xT_sb{i}", [P, KC, S]) for i in range(2)]
        ctx_sb = [sb(f"ctx_sb{i}", [P, KC, SC]) for i in range(2)]
        qT, kT = sb("qT", [CH, S]), sb("kT", [CH, S])
        v_sb = sb("v_sb", [P, TC, CH])
        dsc = sb("dsc", [P, 384])
        ret = sb("ret", [2 * CH, S], F32R)
        x1p = shared(0)
        x1 = [sb(f"x1_{i}", [P, TC, E]) for i in range(2)]
        x1c = [shared(10 + i) for i in range(2)]
        x1T = sb("x1T", [P, KC, P])
        x1T_hi, x1T_lo = sb("x1T_hi", [P, KC, S], F32R), sb("x1T_lo", [P, KC, S], F32R)
        G = sb("G", [P, KC, P])
        G_hi, G_lo = sb("G_hi", [P, KC, P], F32R), sb("G_lo", [P, KC, P], F32R)
        V_hi, V_lo = sb("V_hi", [P, TC, E], F32R), sb("V_lo", [P, TC, E], F32R)
        pr = sb("pr", [P, 384])
        prT_hi, prT_lo = sb("prT_hi", [P, 384], F32R), sb("prT_lo", [P, 384], F32R)
        nmax, ssum, rsum = sb("nmax", [P, TC]), sb("ssum", [P, TC]), sb("rsum", [P, TC])
        asum = shared(3)
        z2 = shared(8)
        hg = shared(4)
        h = [sb(f"h_{i}", [P, TC, E]) for i in range(2)]
        N_sb = [sb(f"N_sb{i}", [P, KC, SC]) for i in range(2)]
        ctx_hi, ctx_lo = sb("ctx_hi", [P, KC, SC], F32R), sb("ctx_lo", [P, KC, SC], F32R)
        Vc_hi = [sb(f"Vc_hi{i}", [P, E], F32R) for i in range(2)]
        Vc_lo = [sb(f"Vc_lo{i}", [P, E], F32R) for i in range(2)]
        hT = sb("hT", [P, KC, S])
        prc = sb("prc", [P, TC, SC])
        prcT_hi, prcT_lo = sb("prcT_hi", [P, S], F32R), sb("prcT_lo", [P, S], F32R)
        nmaxc, ssumc, rsumc = sb("nmaxc", [P, TC]), sb("ssumc", [P, TC]), sb("rsumc", [P, TC])
        csum = shared(5)
        z3 = shared(6)
        h2g = shared(7)
        h2 = [shared(i, late) for i in range(2)]
        z3T_hi, z3T_lo = sb("z3T_hi", [P, KC, S], F32R), sb("z3T_lo", [P, KC, S], F32R)
        fpre = shared(16)
        fsum = shared(17)
        z4 = sb("z4", [P, TC, E])
        z4g, z4b = shared(2, late), shared(9)
        x2p = shared(18)
        x2 = shared(19)
        x2b = [shared(12 + i) for i in range(2)]
        x2T = shared(3, late)
        x2T_hi = [sb(f"x2T_hi{i}", [P, KC, S], F32R) for i in range(2)]
        x2T_lo = [sb(f"x2T_lo{i}", [P, KC, S], F32R) for i in range(2)]
        logit = sb("logit", [P, TC, NBLK])
        lmax = sb("lmax", [P, TC])
        prob = sb("prob", [P, TC, NE])
        top8 = sb("top8", [P, TC, 8])
        top4 = sb("top4", [P, TC, 8])
        struck = sb("struck", [P, TC, NE])
        nmask = sb("nmask", [P, TC, NBLK], BF16)
        maskT = [sb(f"maskT{i}", [NX, S], BF16) for i in range(2)]
        hid_hi, hid_lo = sb("hid_hi", [P, FC, S], F32R), sb("hid_lo", [P, FC, S], F32R)
        ysum = shared(2)
        o_sb = [shared(14 + i) for i in range(2)]
        LN = range(1, 7)
        st = {k: sb(f"st{k}", [P, TC, 6]) for k in LN}
        mv = {k: sb(f"mv{k}", [P, TC, 2]) for k in LN}
        ve = {k: sb(f"ve{k}", [P, TC]) for k in LN}
        rstd = {k: sb(f"rstd{k}", [P, TC]) for k in LN}

        loaded = {n: sem(f"loaded_{n}") for n in
                  ("scal", "attn", "M", "Mc", "xattn", "b1", "w1", "w2", "rows")}
        made = {n: sem(f"made_{n}") for n in
                ("ident", "expand", "fills", "power_of", "decay", "pow_dma", "dmask", "products", "rounded", "rest",
                 "be_wide", "b1_row", "bias_parts", "bias_rows")}
        PRODUCTS = {n: i + 1 for i, n in enumerate(("qkv_w", "o_w", "M", "Mc", "b1_row"))}
        ROUNDED = {n: i + 1 for i, n in enumerate(
            ("qkv_w", "o_hi", "o_full", "M_hi", "M_full", "Mc", "Wcv_hi", "v_hi", "W1_hi", "w1_hi", "w2_hi"))}
        REST = {n: i + 1 for i, n in enumerate(("o_lo", "M_lo", "Wcv_lo", "v_lo", "W1_lo", "w1_lo", "w2_lo"))}
        s_x = [sem(f"s_x{i}") for i in range(2)]
        s_xT = [sem(f"s_xT{i}") for i in range(2)]
        s_ctx = [sem(f"s_ctx{i}") for i in range(2)]
        s_st = [sem(f"s_st{i}") for i in range(2)]
        names = (
            "qkv_mm v sc_mm dsc ret_mm ret retl out1_mm x1p ctxh ctxl ctx_mm Vc Vcl x1t_mm x1T x1Th x1Tl "
            "g_mm G Gl v_mm V Vl s_mm smax ssum pt_mm prT prTl rsum pv_mm asum hg h zt_mm hT cs_mm cmax csm "
            "cpt_mm prcT prcTl rsumc cpv_mm csum h2g h2 x1c z3t_mm z3h z3l w1_mm fpre fsum z4g z4b x2p x2b "
            "x2t_mm x2Th x2Tl lg_mm logit lmax prob top8 top4 struck nmask mt_mm maskT y_mm ysum").split()
        s = {n: sem(f"s_{n}") for n in names}
        s_hmm = [sem(f"s_h_mm{f}") for f in range(4)]
        s_hhi = [sem(f"s_hid_hi{f}") for f in range(4)]
        s_hlo = [sem(f"s_hid_lo{f}") for f in range(4)]
        s_stat = {k: sem(f"s_stat{k}") for k in LN}
        s_mv = {k: sem(f"s_mv{k}") for k in LN}
        s_ve = {k: sem(f"s_ve{k}") for k in LN}
        s_rstd = {k: sem(f"s_rstd{k}") for k in LN}
        s_ln = {k: sem(f"s_ln{k}") for k in LN}

        def after(eng, which, n):
            if not isinstance(n, int) or n > 0:
                eng.wait_ge(which, n)

        def after_apart(eng, which, n, own):
            if not isinstance(n, int):
                n = eng.snap(n)
                eng.wait_ge(own, 1)
            after(eng, which, n)

        def loads(b, par):
            return 8 * (b - par) + 16

        def run(eng, order, steps):
            def turn(i, par):
                for name, lag in order:
                    b = i - lag
                    if not isinstance(b, int) or 0 <= b < NB:
                        steps[name](b, (par + lag) % 2)
            first = LAG + 2 + LAG % 2
            for i in range(first):
                turn(i, i % 2)
            with eng.Fori(first, NB - 1, 2) as i:
                turn(i, 0)
                turn(i + 1, 1)
            for i in range(NB, NB + LAG):
                turn(i, i % 2)

        def ready(eng, b, *what):
            if isinstance(b, int) and b == 0:
                for name, n in what:
                    eng.wait_ge(made[name], n)

        block = ctx.enter_context(nc.Block())

        @block.sync
        def _(sp):
            def rows(w):
                return w.rearrange("(k p) n -> p k n", p=P)

            def fetch(dst, src, group):
                sp.dma_start(dst, src).then_inc(loaded[group], 16)

            def first_loads():
                fetch(scal[:, 0:1], decay_logit.partition_broadcast(P), "scal")
                fetch(scal[:, 1:2], out_scale.partition_broadcast(P), "scal")
                fetch(basis_sb[:, :, :], rows(basisT), "attn")
                for n, w in enumerate((qcT, kcT, vcT, ocT)):
                    fetch(coef[:, :, n * CH:(n + 1) * CH], rows(w), "attn")
                load(0, 0)
                sp.wait_ge(made["decay"], 8)
                line = power_dram.ap()
                sp.dma_start(line.rearrange("o (p q) -> (o p) q", q=3), powers[:, :]).then_inc(made["pow_dma"], 16)
                sp.wait_ge(made["pow_dma"], 16)
                hankel = bass.AP(tensor=line.tensor, offset=0, ap=[[1, P], [1, 256]])
                sp.dma_start(mirror, hankel).then_inc(made["pow_dma"], 16)
                fetch(b1_rest[:, 0, :], fb1.rearrange("(o n) -> o n", o=1), "b1")
                fetch(raw["a"][:, :, :], rows(WqT), "M")
                fetch(raw["b"][:, :, :], rows(WkT), "M")
                fetch(raw["c"][:, :, :], rows(WcqT), "Mc")
                fetch(raw["d"][:, :, :], rows(WckT), "Mc")
                fetch(Wcv_sb[:, :, :], rows(Wcv), "xattn")
                fetch(raw_v[:, :, :], rows(Wv), "xattn")
                fetch(g_col[:, :], gammaC, "xattn")
                fetch(be_col[:, :], betaC, "xattn")
                fetch(raw_1[:, :, :], rows(W1), "xattn")
                for t in range(TC):
                    fetch(g_row[:, t, :], gamma.partition_broadcast(P), "rows")
                    fetch(be_row[:, t, :], beta.partition_broadcast(P), "rows")
                    fetch(b1_row[:, t, :], b1.partition_broadcast(P), "rows")
                    fetch(b2_row[:, t, :], fb2.partition_broadcast(P), "rows")
                    fetch(rb_row[:, t, :], rb.partition_broadcast(P), "rows")
                fetch(rw_sb[:, :, :], rows(rwT), "rows")
                fetch(raw_w1[:, :, :], rows(w1T), "w1")
                fetch(raw_w2, rows(w2T), "w2")
                sp.wait_ge(made["bias_parts"], 3)
                sp.wait_ge(made["expand"], 3)
                for n in range(3):
                    sp.dma_start(expand[NBLK + n:NBLK + n + 1, :, :],
                                 b1_parts[:, n, :].rearrange("o (c m) -> o c m", m=P)).then_inc(made["bias_rows"], 16)

            def load(b, par):
                after(sp, s["x1p"], b - 1)
                sp.dma_start(x_sb[par][:, :, :], x[b].rearrange("(t p) e -> p t e", p=P)).then_inc(s_x[par], 16)
                after(sp, s["qkv_mm"], b - 1)
                sp.dma_start(xT_sb[par][:, :, :], xT[b].rearrange("(k p) t -> p k t", p=P)).then_inc(s_xT[par], 16)
                after(sp, s["ctx_mm"], b - 1)
                sp.dma_start(ctx_sb[par][:, :, :], ctxT[b].rearrange("(k p) t -> p k t", p=P)).then_inc(s_ctx[par], 16)

            def store(b, par):
                after(sp, s_ln[6], b + 1)
                sp.dma_start(out[b].rearrange("(t p) e -> p t e", p=P), o_sb[par][:, :, :]).then_inc(s_st[par], 16)

            first_loads()
            lag = dict(TURN["vector"])["ln6"]

            def turn(i, par):
                if not isinstance(i, int) or 0 < i < NB:
                    load(i, par)
                j = i - lag - 1
                if not isinstance(j, int) or 0 <= j < NB:
                    store(j, (par + lag + 1) % 2)

            first = LAG + 2 + LAG % 2
            for i in range(first):
                turn(i, i % 2)
            with sp.Fori(first, NB - 1, 2) as i:
                turn(i, 0)
                turn(i + 1, 1)
            for i in range(NB, NB + lag + 1):
                turn(i, i % 2)
            for par in range(2):
                sp.wait_ge(s_st[par], 16 * (NB // 2))

        @block.gpsimd
        def _(pool):
            pool.memset(scal[:, 2:3], 2.718281828459045).then_inc(made["decay"], 1)
            pool.iota(power_step[:, :], pattern=[[1, 3]], base=-P, channel_multiplier=3).then_inc(made["power_of"], 1)
            pool.wait_ge(made["power_of"], 1)
            pool.tensor_copy(power_of[:, :], power_step[:, :]).then_inc(made["power_of"], 1)
            pool.wait_ge(loaded["scal"], 32)
            pool.tensor_scalar(scal[:, 3:4], scal[:, 0:1], -1.0, 0.0, ALU.mult, ALU.add).then_inc(made["decay"], 1)
            pool.wait_ge(made["decay"], 2)
            pool.tensor_tensor(scal[:, 4:5], scal[:, 2:3], scal[:, 3:4], ALU.pow).then_inc(made["decay"], 1)
            pool.memset(ident[:, :], 0.0).then_inc(made["ident"], 1)
            pool.wait_ge(made["ident"], 1)
            pool.affine_select(out=ident[:, :], in_=ident[:, :], compare_op=ALU.not_equal, fill=1.0, base=0,
                               pattern=[[-1, P]], channel_multiplier=1).then_inc(made["ident"], 1)
            pool.wait_ge(made["decay"], 6)
            pool.tensor_tensor(powers[:, :], decay_col[:, :], power_of[:, :], ALU.pow).then_inc(made["decay"], 1)
            pool.wait_ge(made["decay"], 7)
            pool.affine_select(out=powers[:, :], in_=powers[:, :], compare_op=ALU.is_ge, fill=0.0, base=-P,
                               pattern=[[1, 3]], channel_multiplier=3).then_inc(made["decay"], 1)
            pool.memset(half[:, :], -0.5).then_inc(made["fills"], 1)
            pool.memset(eps_block[:, :], EPS_BLOCK).then_inc(made["fills"], 1)
            pool.memset(eps_xattn[:, :], EPS_XATTN).then_inc(made["fills"], 1)
            pool.memset(causal_bf[:, :], 0.0).then_inc(made["ident"], 1)
            pool.wait_ge(made["ident"], 3)
            pool.affine_select(out=causal_bf[:, :], in_=causal_bf[:, :], compare_op=ALU.is_ge, fill=-BIG, base=0,
                               pattern=[[-1, P]], channel_multiplier=1).then_inc(made["ident"], 1)
            pool.tensor_copy(ident_bf[:, :], ident[:, :]).then_inc(made["ident"], 1)
            ex = expand[0:NBLK, :, :]
            pool.memset(expand[:, :, :], 1.0).then_inc(made["expand"], 1)
            pool.wait_ge(made["expand"], 1)
            pool.affine_select(out=ex, in_=ex, compare_op=ALU.is_ge, fill=0.0, base=0,
                               pattern=[[P, FC], [1, P]], channel_multiplier=-BLK).then_inc(made["expand"], 1)
            pool.wait_ge(made["expand"], 2)
            pool.affine_select(out=ex, in_=ex, compare_op=ALU.is_ge, fill=0.0, base=BLK - 1,
                               pattern=[[-P, FC], [-1, P]], channel_multiplier=BLK).then_inc(made["expand"], 1)
            for par in range(2):
                pool.memset(maskT[par][:, :], 1.0).then_inc(made["fills"], 1)
            pool.memset(prob[:, :, :], -1.0).then_inc(made["fills"], 1)
            pool.memset(top4[:, :, :], -1.0).then_inc(made["fills"], 1)
            pool.wait_ge(made["fills"], 3)
            own = made["fills"]

            def norm_scale(k, b, eps):
                after(pool, s_mv[k], b + 1)
                pool.tensor_tensor(ve[k][:, :], mv[k][:, :, 1], eps[:, :], ALU.add).then_inc(s_ve[k], 1)
                after(pool, s_ve[k], b + 1)
                pool.tensor_tensor(rstd[k][:, :], ve[k][:, :], half[:, :], ALU.pow).then_inc(s_rstd[k], 1)

            def affine(z, zg, out_t, s_g, s_b, b):
                pool.tensor_tensor(zg[:, :, :], z[:, :, :], g_row[:, :, :], ALU.mult).then_inc(s_g, 1)
                after(pool, s_g, b + 1)
                pool.tensor_tensor(out_t[:, :, :], zg[:, :, :], be_row[:, :, :], ALU.add).then_inc(s_b, 1)

            def cx(b, par):
                after(pool, s["ctxh"], b + 1)
                pool.tensor_tensor(ctx_lo[:, :, :], ctx_sb[par][:, :, :], ctx_hi[:, :, :].bitcast(F32), ALU.subtract)\
                    .then_inc(s["ctxl"], 1)

            def out1(b, par):
                norm_scale(1, b, eps_block)

            def pv(b, par):
                norm_scale(2, b, eps_xattn)

            def ln2(b, par):
                if isinstance(b, int) and b == 0:
                    pool.wait_ge(loaded["rows"], 16 * (5 * TC + 1))
                after(pool, s_ln[2], b + 1)
                after(pool, s["csum"], b - 1)
                affine(z2, hg, h[par], s["hg"], s["h"], b)

            def cpv(b, par):
                norm_scale(3, b, eps_xattn)

            def ln3(b, par):
                after(pool, s_ln[3], b + 1)
                after(pool, s["fsum"], b - 1)
                affine(z3, h2g, h2[par], s["h2g"], s["h2"], b)
                ready(pool, b, ("rest", REST["w2_lo"]))
                after_apart(pool, s_ln[1], b + 1, own)
                after(pool, s["x2p"], b - 1)
                pool.tensor_scalar(x1c[par][:, :, :], x1[par][:, :, :], 1.0, 0.0, ALU.mult, ALU.add)\
                    .then_inc(s["x1c"], 1)

            def w1(b, par):
                norm_scale(4, b, eps_xattn)

            def ln4(b, par):
                after(pool, s_ln[4], b + 1)
                after(pool, s["x2p"], b)
                affine(z4, z4g, z4b, s["z4g"], s["z4b"], b)

            def x2sum(b, par):
                norm_scale(5, b, eps_block)

            def ln5(b, par):
                after(pool, s_ln[5], b + 1)
                after(pool, s["ysum"], b - 1)
                pool.tensor_tensor(x2b[par][:, :, :], x2[:, :, :], b2_row[:, :, :], ALU.add).then_inc(s["x2b"], 1)

            def y(b, par):
                norm_scale(6, b, eps_block)

            run(pool, TURN["gpsimd"], dict(
                cx=cx, out1=out1, pv=pv, ln2=ln2, cpv=cpv, ln3=ln3, w1=w1, ln4=ln4, x2sum=x2sum, ln5=ln5,
                y1=y))

        @block.tensor
        def _(pe):
            def product(out_ap, terms):
                for n, (lhs, rhs) in enumerate(terms):
                    mm = pe.matmul(out_ap, lhs, rhs, start=(n == 0), stop=(n == len(terms) - 1))
                return mm

            def split(lhs_hi, lhs_lo, rhs_hi, rhs_lo):
                return [(lhs_hi, rhs_hi), (lhs_hi, rhs_lo), (lhs_lo, rhs_hi)]

            def cols(c, n=P):
                return slice(c * n, (c + 1) * n)

            pe.wait_ge(loaded["attn"], 16 * 5)
            for c in range(KC):
                mm = product(pA[:, 192 * c:192 * c + 192],
                             [(basis_sb[:, k, cols(c)], coef[:, k, 0:3 * CH]) for k in range(KC)])
            mm.then_inc(made["products"], 1)
            product(pB[0:CH, 0:E], [(coef[:, k, 3 * CH:4 * CH], basis_sb[:, k, :]) for k in range(KC)])\
                .then_inc(made["products"], 1)

            def weights():
                pe.wait_ge(loaded["M"], 32)
                for c in range(KC):
                    mm = product(pC[:, cols(c, E)], [(raw["a"][:, k, cols(c)], raw["b"][:, k, :]) for k in range(KC)])
                mm.then_inc(made["products"], 1)
                pe.wait_ge(loaded["Mc"], 32)
                for c in range(KC):
                    mm = product(pD[:, cols(c, E)], [(raw["d"][:, k, cols(c)], raw["c"][:, k, :]) for k in range(KC)])
                mm.then_inc(made["products"], 1)
                pe.wait_ge(loaded["xattn"], 80)
                pe.wait_ge(made["be_wide"], 1)
                product(pE[:, 0:E], [(be_wide[:, k, :], raw_1[:, k, :]) for k in range(KC)])\
                    .then_inc(made["products"], 1)

            def qkv(b, par):
                ready(pe, b, ("rounded", ROUNDED["qkv_w"]))
                pe.wait_ge(s_xT[par], loads(b, par))
                after(pe, s["x1p"], b)
                product(pA[:, 0:S], [(qkv_w[:, k, 0:2 * CH], xT_sb[par][:, k, :]) for k in range(KC)])
                for c in range(TC):
                    mm = product(pA[:, S + CH * c:S + CH * c + CH],
                                 [(xT_sb[par][:, k, cols(c)], qkv_w[:, k, 2 * CH:3 * CH]) for k in range(KC)])
                mm.then_inc(s["qkv_mm"], 1)

            def sc(b, par):
                after(pe, s["v"], b + 1)
                product(pA[:, 0:256], [(kT[:, P:S], qT[:, :])])
                product(pA[:, 256:384], [(kT[:, 0:P], qT[:, 0:P])]).then_inc(s["sc_mm"], 1)

            def ret_(b, par):
                after(pe, s["dsc"], b + 1)
                pe.matmul(pA[0:CH, 0:S], v_sb[:, 1, :], dsc[:, 0:256], start=True, stop=False)
                pe.matmul(pA[0:CH, 0:P], v_sb[:, 0, :], dsc[:, 256:384], start=False, stop=True)\
                    .then_inc(s["ret_mm"], 1)

            def out1(b, par):
                ready(pe, b, ("rest", REST["o_lo"]))
                after(pe, s["retl"], b + 1)
                for c in range(TC):
                    mm = product(pA[:, cols(c, E)], [(ret[:, cols(c)], ow_hi[:, :]), (ret[0:CH, cols(c)], ow_lo[:, :])])
                mm.then_inc(s["out1_mm"], 1)
                if isinstance(b, int) and b == 0:
                    weights()

            def ctx_(b, par):
                ready(pe, b, ("rounded", ROUNDED["Mc"]), ("rest", REST["Wcv_lo"]))
                pe.wait_ge(s_ctx[par], loads(b, par))
                after(pe, s["Vl"], b)
                after(pe, s["ctxl"], b + 1)
                for c in range(KC):
                    product(pV[:, SC * c:SC * c + SC],
                            [(McT[:, k, cols(c)], ctx_sb[par][:, k, :]) for k in range(KC)])
                terms = []
                for k in range(KC):
                    terms += split(ctx_hi[:, k, :], ctx_lo[:, k, :], Wcv_hi[:, k, :], Wcv_lo[:, k, :])
                product(pV[0:SC, 256:512], terms).then_inc(s["ctx_mm"], 1)

            def turned(bank_ap, src):
                for k in range(KC):
                    for c in range(TC):
                        mm = pe.transpose(bank_ap[:, S * k + P * c:S * k + P * c + P], src[:, c, cols(k)], ident[:, :])
                return mm

            def x1t(b, par):
                ready(pe, b, ("ident", 5))
                after(pe, s_ln[1], b + 1)
                after(pe, s["asum"], b)
                turned(pB, x1[par]).then_inc(s["x1t_mm"], 1)

            def g(b, par):
                ready(pe, b, ("rest", REST["M_lo"]))
                after(pe, s["x1T"], b + 1)
                for c in range(KC):
                    terms = []
                    for k in range(KC):
                        terms += split(M_hi[:, k, cols(c)], M_lo[:, k, cols(c)], x1T_hi[:, k, :], x1T_lo[:, k, :])
                    mm = product(pB[:, cols(c, S)], terms)
                mm.then_inc(s["g_mm"], 1)

            def v(b, par):
                ready(pe, b, ("rest", REST["v_lo"]))
                after(pe, s["x1Tl"], b + 1)
                after(pe, s["Vcl"], b + 1)
                for c in range(TC):
                    terms = []
                    for k in range(KC):
                        terms += split(x1T_hi[:, k, cols(c)], x1T_lo[:, k, cols(c)], Wv_hi[:, k, :], Wv_lo[:, k, :])
                    mm = product(pV[:, cols(c, E)], terms)
                mm.then_inc(s["v_mm"], 1)

            def s_(b, par):
                after(pe, s["Gl"], b + 1)
                terms = []
                for k in range(KC):
                    terms += split(G_hi[:, k, :], G_lo[:, k, :], x1T_hi[:, k, :], x1T_lo[:, k, :])
                for n, (lhs, rhs) in enumerate(terms):
                    pe.matmul(pB[:, 0:256], lhs, rhs, start=(n == 0), stop=False)
                pe.matmul(pB[:, P:256], ident_bf[:, :], causal_bf[:, :], start=False, stop=True)
                for k in range(KC):
                    pe.matmul(pB[:, 256:384], G[:, k, :], x1T[:, k, :], start=(k == 0), stop=False)
                pe.matmul(pB[:, 256:384], ident_bf[:, :], causal_bf[:, :], start=False, stop=True)\
                    .then_inc(s["s_mm"], 1)

            def pt(b, par):
                after(pe, s["ssum"], b + 1)
                for c in range(3):
                    mm = pe.transpose(pB[:, cols(c)], pr[:, cols(c)], ident[:, :])
                mm.then_inc(s["pt_mm"], 1)

            def pv(b, par):
                after(pe, s["prTl"], b + 1)
                after(pe, s["Vl"], b + 1)

                def term(c, block):
                    return split(prT_hi[:, block], prT_lo[:, block], V_hi[:, c, :], V_lo[:, c, :])

                product(pB[:, 0:256], term(0, slice(256, 384)))
                product(pB[:, 256:512], term(0, cols(0)) + term(1, cols(1))).then_inc(s["pv_mm"], 1)

            def zt(b, par):
                ready(pe, b, ("rounded", ROUNDED["M_full"]))
                after(pe, s_ln[2], b + 1)
                after(pe, s["csum"], b)
                turned(pC, z2).then_inc(s["zt_mm"], 1)

            def cs(b, par):
                after(pe, s["hT"], b + 1)
                after(pe, s["Vc"], b + 1)
                for c in range(TC):
                    mm = product(pC[:, SC * c:SC * c + SC],
                                 [(hT[:, k, cols(c)], N_sb[par][:, k, :]) for k in range(KC)])
                mm.then_inc(s["cs_mm"], 1)

            def cpt(b, par):
                after(pe, s["csm"], b + 1)
                for c in range(TC):
                    mm = pe.transpose(pC[0:SC, cols(c)], prc[:, c, :], ident[:, :])
                mm.then_inc(s["cpt_mm"], 1)

            def cpv(b, par):
                after(pe, s["prcTl"], b + 1)
                after(pe, s["Vcl"], b + 1)
                for c in range(TC):
                    mm = product(pC[:, cols(c, E)], split(prcT_hi[0:SC, cols(c)], prcT_lo[0:SC, cols(c)],
                                                          Vc_hi[par][0:SC, :], Vc_lo[par][0:SC, :]))
                mm.then_inc(s["cpv_mm"], 1)

            def z3t(b, par):
                ready(pe, b, ("rounded", ROUNDED["Mc"]))
                after(pe, s_ln[3], b + 1)
                after(pe, s["fpre"], b)
                turned(pD, z3).then_inc(s["z3t_mm"], 1)

            def w1(b, par):
                ready(pe, b, ("rest", REST["W1_lo"]))
                after(pe, s["z3l"], b + 1)
                for c in range(TC):
                    terms = []
                    for k in range(KC):
                        terms += split(z3T_hi[:, k, cols(c)], z3T_lo[:, k, cols(c)], W1_hi[:, k, :], W1_lo[:, k, :])
                    mm = product(pD[:, cols(c, E)], terms)
                mm.then_inc(s["w1_mm"], 1)

            def x2t(b, par):
                ready(pe, b, ("b1_row", 3))
                after(pe, s_ln[5], b + 1)
                after(pe, s["maskT"], b)
                turned(pE, x2).then_inc(s["x2t_mm"], 1)

            def lg(b, par):
                if isinstance(b, int) and b == 0:
                    pe.wait_ge(loaded["rows"], 16 * (5 * TC + 1))
                after(pe, s["x2Tl"], b + 1)
                for c in range(TC):
                    mm = product(pE[:, NBLK * c:NBLK * c + NBLK],
                                 [(x2T[:, k, cols(c)], rw_sb[:, k, :]) for k in range(KC)])
                mm.then_inc(s["lg_mm"], 1)

            def mt(b, par):
                after(pe, s["nmask"], b + 1)
                for c in range(TC):
                    mm = pe.transpose(pE[0:NBLK, cols(c, 64)].bitcast(BF16), nmask[:, c, :], ident_bf[:, :])
                mm.then_inc(s["mt_mm"], 1)

            def hidden(f):
                def step(b, par):
                    ready(pe, b, ("rest", REST["w1_lo"]))
                    if isinstance(b, int) and b == 0:
                        pe.wait_ge(made["bias_rows"], 48)
                    after(pe, s["x2Tl"], b + 1)
                    if f == 0:
                        after(pe, s["ysum"], b)
                    elif f == 1:
                        after(pe, s_hlo[3], b)
                    else:
                        after(pe, s_hlo[f - 2], b + 1)
                    for n in range(2):
                        c = 2 * f + n
                        terms = []
                        for k in range(KC):
                            terms += split(w1_hi[:, k, cols(c)], w1_lo[:, k, cols(c)],
                                           x2T_hi[par][:, k, :], x2T_lo[par][:, k, :])
                        for m, (lhs, rhs) in enumerate(terms):
                            pe.matmul(pH[f % 2][:, cols(n, S)], lhs, rhs, start=(m == 0), stop=False)
                        after(pe, s["maskT"], b + 1)
                        mm = pe.matmul(pH[f % 2][:, cols(n, S)], expand[:, c, :], maskT[par][:, :], start=False,
                                       stop=True)
                    mm.then_inc(s_hmm[f], 1)
                return step

            def output(c):
                def step(b, par):
                    ready(pe, b, ("rest", REST["w2_lo"]))
                    after(pe, s_hlo[2], b + 1)
                    terms = []
                    for k in range(FC):
                        terms += split(hid_hi[:, k, cols(c)], hid_lo[:, k, cols(c)], w2_hi[:, k, :], w2_lo[:, k, :])
                    for n, (lhs, rhs) in enumerate(terms):
                        if n == 18 and c == 0:
                            after(pe, s_hlo[3], b + 1)
                        mm = pe.matmul(pH[0][:, cols(c, E)], lhs, rhs, start=(n == 0), stop=(n == len(terms) - 1))
                    if c == TC - 1:
                        mm.then_inc(s["y_mm"], 1)
                return step

            run(pe, TURN["tensor"], dict(
                qkv=qkv, sc=sc, ret=ret_, out1=out1, ctx=ctx_, x1t=x1t, g=g, v=v, s=s_, pt=pt, pv=pv, zt=zt,
                cs=cs, cpt=cpt, cpv=cpv, z3t=z3t, w1=w1, x2t=x2t, lg=lg, mt=mt, h0=hidden(0), h1=hidden(1),
                h2=hidden(2), h3=hidden(3), y0=output(0), y1=output(1)))

        def halves(bank_t):
            return bank_t[:, :].rearrange("p (k t) -> p k t", k=KC)

        def flat(t):
            return t[:, :, :].rearrange("p a b -> p (a b)")

        @block.scalar
        def _(act):
            done = made["rounded"]
            act.wait_ge(made["products"], PRODUCTS["qkv_w"])
            act.activation(flat(qkv_w), pA[:, 0:384], ACT.Copy).then_inc(done, 1)
            act.wait_ge(made["products"], PRODUCTS["o_w"])
            act.wait_ge(loaded["scal"], 32)
            act.activation(ow_hi[0:CH, :], pB[0:CH, 0:E], ACT.Copy, scale=scal[0:CH, 1:2])
            act.activation(ow_hi[CH:2 * CH, :], pB[0:CH, 0:E], ACT.Copy, scale=scal[0:CH, 1:2]).then_inc(done, 1)
            act.activation(o_wT[:, :], pB[0:CH, 0:E], ACT.Copy, scale=scal[0:CH, 1:2]).then_inc(done, 1)

            def weights():
                act.wait_ge(made["products"], PRODUCTS["M"])
                act.activation(flat(M_hi), pC[:, :], ACT.Copy, scale=SCALE).then_inc(done, 1)
                act.activation(flat(z4), pC[:, :], ACT.Copy, scale=SCALE).then_inc(done, 1)
                act.wait_ge(made["products"], PRODUCTS["Mc"])
                act.activation(flat(McT), pD[:, :], ACT.Copy, scale=SCALE).then_inc(done, 1)
                act.wait_ge(loaded["xattn"], 80)
                act.activation(flat(Wcv_hi), flat(Wcv_sb), ACT.Copy).then_inc(done, 1)
                act.activation(flat(Wv_hi), flat(raw_v), ACT.Copy).then_inc(done, 1)
                for k in range(KC):
                    a = act.activation(W1_hi[:, k, :], raw_1[:, k, :], ACT.Copy, scale=g_col[:, k:k + 1])
                a.then_inc(done, 1)

            def ffn_weights(rounded, raw_w, group):
                act.wait_ge(loaded[group], 16)
                act.activation(flat(rounded), flat(raw_w), ACT.Copy).then_inc(done, 1)

            def copy(dst, src, after_sem, n, done_sem):
                after(act, after_sem, n)
                act.activation(dst, src, ACT.Copy).then_inc(done_sem, 1)

            def qkv(b, par):
                after(act, s["qkv_mm"], b + 1)
                act.activation(qT[:, :], pA[0:CH, 0:S], ACT.Copy)
                act.activation(kT[:, :], pA[CH:2 * CH, 0:S], ACT.Copy)
                act.activation(flat(v_sb), pA[:, S:S + TC * CH], ACT.Copy).then_inc(s["v"], 1)

            def ret_(b, par):
                copy(ret[0:CH, :], pA[0:CH, 0:S], s["ret_mm"], b + 1, s["ret"])
                if isinstance(b, int) and b == 0:
                    weights()

            def cx(b, par):
                act.wait_ge(s_ctx[par], loads(b, par))
                after(act, s["ctx_mm"], b)
                act.activation(flat(ctx_hi), flat(ctx_sb[par]), ACT.Copy).then_inc(s["ctxh"], 1)

            def ctx_(b, par):
                after(act, s["cpv_mm"], b - 1)
                after(act, s["ctx_mm"], b + 1)
                act.activation(flat(N_sb[par]), pV[:, 0:KC * SC], ACT.Copy)
                act.activation(Vc_hi[par][0:SC, :], pV[0:SC, 256:512], ACT.Copy).then_inc(s["Vc"], 1)

            def x1t(b, par):
                copy(flat(x1T_hi), pB[:, :], s["x1t_mm"], b + 1, s["x1Th"])
                after(act, s["x1Tl"], b + 1)
                act.activation(x1T[:, :, :], halves(pB)[:, :, 0:P], ACT.Copy).then_inc(s["x1T"], 1)

            def g(b, par):
                after(act, s["g_mm"], b + 1)
                act.activation(G[:, :, :], halves(pB)[:, :, 0:P], ACT.Copy)
                act.activation(G_hi[:, :, :], halves(pB)[:, :, P:S], ACT.Copy).then_inc(s["G"], 1)
                if isinstance(b, int) and b == 0:
                    ffn_weights(w1_hi, raw_w1, "w1")

            def v(b, par):
                copy(flat(V_hi), pV[:, :], s["v_mm"], b + 1, s["V"])

            def softmax(b, blocks, bank_t, out_ap, neg, sums, s_max, s_sum):
                after(act, s_max, b + 1)
                for c, (lo, hi) in enumerate(blocks):
                    e = act.activation(out_ap(c), bank_t[:, lo:hi], ACT.Exp, bias=neg[:, c:c + 1],
                                       accum_out=sums[:, c:c + 1])
                e.then_inc(s_sum, 1)

            def s_(b, par):
                blocks = [(256, 384), (0, 256)]
                after(act, s["rsum"], b)
                softmax(b, blocks, pB, lambda c: pr[:, blocks[c][0]:blocks[c][1]], nmax, ssum, s["smax"], s["ssum"])

            def pt(b, par):
                copy(prT_hi[:, :], pB[:, 0:384], s["pt_mm"], b + 1, s["prT"])
                if isinstance(b, int) and b == 0:
                    ffn_weights(w2_hi, raw_w2, "w2")

            def zt(b, par):
                after(act, s["zt_mm"], b + 1)
                for k in range(KC):
                    a = act.activation(hT[:, k, :], pC[:, S * k:S * k + S], ACT.Identity,
                                       scale=g_col[:, k:k + 1], bias=be_col[:, k:k + 1])
                a.then_inc(s["hT"], 1)

            def cs(b, par):
                after(act, s["rsumc"], b)
                softmax(b, [(SC * c, SC * c + SC) for c in range(TC)], pC, lambda c: prc[:, c, :], nmaxc, ssumc,
                        s["cmax"], s["csm"])

            def cpt(b, par):
                copy(prcT_hi[0:SC, :], pC[0:SC, 0:S], s["cpt_mm"], b + 1, s["prcT"])

            def z3t(b, par):
                copy(flat(z3T_hi), pD[:, :], s["z3t_mm"], b + 1, s["z3h"])

            def x2t(b, par):
                after(act, s_hmm[3], b - 1)
                after(act, s["x2t_mm"], b + 1)
                act.activation(flat(x2T), pE[:, :], ACT.Copy)
                act.activation(flat(x2T_hi[par]), pE[:, :], ACT.Copy).then_inc(s["x2Th"], 1)

            def lg(b, par):
                after(act, s["lmax"], b + 1)
                after(act, s["struck"], b)
                for c in range(TC):
                    a = act.activation(prob[:, c, 0:NBLK], logit[:, c, :], ACT.Exp, bias=lmax[:, c:c + 1])
                a.then_inc(s["prob"], 1)

            def mt(b, par):
                after(act, s_hmm[3], b - 1)
                copy(maskT[par][0:NBLK, :], pE[0:NBLK, 0:P].bitcast(BF16), s["mt_mm"], b + 1, s["maskT"])

            def hidden(f):
                def step(b, par):
                    after(act, s["y_mm"], b)
                    after(act, s_hmm[f], b + 1)
                    act.activation(hid_hi[:, 2 * f:2 * f + 2, :].rearrange("p a b -> p (a b)"), pH[f % 2][:, :],
                                   ACT.Relu).then_inc(s_hhi[f], 1)
                return step

            run(act, TURN["scalar"], dict(
                cx=cx, qkv=qkv, ret=ret_, ctx=ctx_, x1t=x1t, g=g, v=v, s=s_, pt=pt, zt=zt, cs=cs, cpt=cpt,
                z3t=z3t, x2t=x2t, lg=lg, mt=mt, h0=hidden(0), h1=hidden(1), h2=hidden(2), h3=hidden(3)))

        @block.vector
        def _(dve):
            dve.wait_ge(made["decay"], 3)
            dve.tensor_scalar(scal[:, 5:6], scal[:, 4:5], 1.0, None, ALU.add).then_inc(made["decay"], 1)
            dve.wait_ge(made["decay"], 4)
            dve.reciprocal(scal[:, 6:7], scal[:, 5:6]).then_inc(made["decay"], 1)
            dve.wait_ge(made["decay"], 5)
            dve.wait_ge(made["power_of"], 2)
            dve.tensor_scalar(decay_col[:, :], power_of[:, :], 0.0, scal[:, 6:7], ALU.mult, ALU.add)\
                .then_inc(made["decay"], 1)
            parts = made["bias_parts"]
            dve.wait_ge(loaded["b1"], 16)
            dve.tensor_copy(b1_parts[:, 0, :], b1_rest[:, 0, :]).then_inc(parts, 1)
            dve.wait_ge(parts, 1)
            dve.tensor_tensor(b1_rest[:, 1, :], b1_rest[:, 0, :], b1_parts[:, 0, :], ALU.subtract)\
                .then_inc(made["b1_row"], 1)
            dve.wait_ge(made["b1_row"], 1)
            dve.tensor_copy(b1_parts[:, 1, :], b1_rest[:, 1, :]).then_inc(parts, 1)
            dve.wait_ge(parts, 2)
            dve.tensor_tensor(b1_parts[:, 2, :], b1_rest[:, 1, :], b1_parts[:, 1, :], ALU.subtract)\
                .then_inc(parts, 1)
            dve.wait_ge(made["rounded"], ROUNDED["o_full"])
            dve.tensor_tensor(ow_lo[:, :], o_wT[:, :], ow_hi[0:CH, :].bitcast(F32), ALU.subtract)\
                .then_inc(made["rest"], 1)
            dve.wait_ge(made["pow_dma"], 32)
            dve.tensor_copy(dmask[:, 0:256], work[:, 2, 255::-1]).then_inc(made["dmask"], 1)
            dve.tensor_copy(dmask[:, 256:384], work[:, 2, P - 1::-1]).then_inc(made["dmask"], 1)
            dve.wait_ge(made["dmask"], 2)
            own = made["dmask"]

            def weights():
                dve.wait_ge(loaded["xattn"], 80)
                dve.wait_ge(loaded["rows"], 16 * (5 * TC + 1))
                for k in range(KC):
                    t = dve.tensor_scalar(be_wide[:, k, :], g_row[:, 0, 0:P], 0.0, be_col[:, k:k + 1],
                                          ALU.mult, ALU.add)
                t.then_inc(made["be_wide"], 1)
                dve.wait_ge(made["rounded"], ROUNDED["M_full"])
                dve.tensor_tensor(flat(M_lo), flat(z4), flat(M_hi).bitcast(F32), ALU.subtract)\
                    .then_inc(made["rest"], 1)
                dve.wait_ge(made["rounded"], ROUNDED["Wcv_hi"])
                dve.tensor_tensor(flat(Wcv_lo), flat(Wcv_sb), flat(Wcv_hi).bitcast(F32), ALU.subtract)\
                    .then_inc(made["rest"], 1)
                dve.wait_ge(made["rounded"], ROUNDED["v_hi"])
                dve.tensor_tensor(flat(Wv_lo), flat(raw_v), flat(Wv_hi).bitcast(F32), ALU.subtract)\
                    .then_inc(made["rest"], 1)
                dve.wait_ge(made["rounded"], ROUNDED["W1_hi"])
                for k in range(KC):
                    t = dve.scalar_tensor_tensor(W1_lo[:, k, :], raw_1[:, k, :], g_col[:, k:k + 1],
                                                 W1_hi[:, k, :].bitcast(F32), ALU.mult, ALU.subtract)
                t.then_inc(made["rest"], 1)
                dve.wait_ge(made["products"], PRODUCTS["b1_row"])
                for c in range(TC):
                    dve.tensor_tensor(b1_row[:, c, :], pE[:, 0:E], b1_row[:, c, :], ALU.add)\
                        .then_inc(made["b1_row"], 1)

            def ffn_weights(lo, raw_w, hi, name):
                dve.wait_ge(made["rounded"], ROUNDED[name])
                dve.tensor_tensor(flat(lo), flat(raw_w), flat(hi).bitcast(F32), ALU.subtract)\
                    .then_inc(made["rest"], 1)

            def rest(lo, bank_t, hi, s_hi, b, s_lo):
                after(dve, s_hi, b + 1)
                dve.tensor_tensor(flat(lo), bank_t[:, :], flat(hi).bitcast(F32), ALU.subtract).then_inc(s_lo, 1)

            def stats(k, src, s_src, b):
                after(dve, s_src, b + 1)
                for c in range(TC):
                    t = dve.bn_stats(st[k][:, c, :], src[:, c, :])
                t.then_inc(s_stat[k], 1)
                after_apart(dve, s_stat[k], b + 1, own)
                for c in range(TC):
                    t = dve.bn_aggr(mv[k][:, c, :], st[k][:, c, :])
                t.then_inc(s_mv[k], 1)

            def normed(k, dst, src, b):
                after(dve, s_rstd[k], b + 1)
                for c in range(TC):
                    t = dve.tensor_scalar(dst[:, c, :], src[:, c, :], mv[k][:, c, 0:1], rstd[k][:, c:c + 1],
                                          ALU.subtract, ALU.mult)
                t.then_inc(s_ln[k], 1)

            def sc(b, par):
                after(dve, s["sc_mm"], b + 1)
                dve.tensor_tensor(dsc[:, :], pA[:, 0:384], dmask[:, :], ALU.mult).then_inc(s["dsc"], 1)

            def ret_(b, par):
                after(dve, s["ret"], b + 1)
                dve.tensor_tensor(ret[CH:2 * CH, :], pA[0:CH, 0:S], ret[0:CH, :].bitcast(F32), ALU.subtract)\
                    .then_inc(s["retl"], 1)

            def ctx_(b, par):
                after(dve, s["Vc"], b + 1)
                dve.tensor_tensor(Vc_lo[par][0:SC, :], pV[0:SC, 256:512], Vc_hi[par][0:SC, :].bitcast(F32),
                                  ALU.subtract).then_inc(s["Vcl"], 1)

            def g(b, par):
                after(dve, s["G"], b + 1)
                dve.tensor_tensor(G_lo[:, :, :], halves(pB)[:, :, P:S], G_hi[:, :, :].bitcast(F32), ALU.subtract)\
                    .then_inc(s["Gl"], 1)

            def v(b, par):
                rest(V_lo, pV, V_hi, s["V"], b, s["Vl"])

            def pt(b, par):
                after(dve, s["prT"], b + 1)
                dve.tensor_tensor(prT_lo[:, :], pB[:, 0:384], prT_hi[:, :].bitcast(F32), ALU.subtract)\
                    .then_inc(s["prTl"], 1)

            def cpt(b, par):
                after(dve, s["prcT"], b + 1)
                dve.tensor_tensor(prcT_lo[0:SC, :], pC[0:SC, 0:S], prcT_hi[0:SC, :].bitcast(F32), ALU.subtract)\
                    .then_inc(s["prcTl"], 1)

            def out1(b, par):
                dve.wait_ge(s_x[par], loads(b, par))
                after(dve, s["out1_mm"], b + 1)
                dve.tensor_tensor(flat(x1p), pA[:, :], flat(x_sb[par]), ALU.add).then_inc(s["x1p"], 1)
                stats(1, x1p, s["x1p"], b)

            def ln1(b, par):
                after(dve, s["x1c"], b - 1)
                after(dve, s["asum"], b - 1)
                normed(1, x1[par], x1p, b)
                if isinstance(b, int) and b == 0:
                    weights()

            def x1t(b, par):
                rest(x1T_lo, pB, x1T_hi, s["x1Th"], b, s["x1Tl"])

            def s_(b, par):
                after(dve, s["s_mm"], b + 1)
                dve.tensor_reduce(nmax[:, 0:1], pB[:, 256:384], AX.X, ALU.max, negate=True)
                dve.tensor_reduce(nmax[:, 1:2], pB[:, 0:256], AX.X, ALU.max, negate=True).then_inc(s["smax"], 1)
                if isinstance(b, int) and b == 0:
                    ffn_weights(w1_lo, raw_w1, w1_hi, "w1_hi")

            def pv(b, par):
                after(dve, s["ssum"], b + 1)
                dve.reciprocal(rsum[:, :], ssum[:, :]).then_inc(s["rsum"], 1)
                after(dve, s["rsum"], b + 1)
                after(dve, s["pv_mm"], b + 1)
                for c in range(TC):
                    t = dve.scalar_tensor_tensor(asum[:, c, :], pB[:, E * c:E * c + E], rsum[:, c:c + 1],
                                                 x1[par][:, c, :], ALU.mult, ALU.add)
                t.then_inc(s["asum"], 1)
                stats(2, asum, s["asum"], b)

            def ln2(b, par):
                after(dve, s["zt_mm"], b)
                after(dve, s["h"], b)
                normed(2, z2, asum, b)
                if isinstance(b, int) and b == 0:
                    ffn_weights(w2_lo, raw_w2, w2_hi, "w2_hi")

            def cs(b, par):
                after(dve, s["cs_mm"], b + 1)
                dve.tensor_reduce(nmaxc[:, :], pC[:, 0:TC * SC].rearrange("p (t k) -> p t k", t=TC), AX.X, ALU.max,
                                  negate=True).then_inc(s["cmax"], 1)

            def cpv(b, par):
                after(dve, s["csm"], b + 1)
                dve.reciprocal(rsumc[:, :], ssumc[:, :]).then_inc(s["rsumc"], 1)
                after(dve, s["rsumc"], b + 1)
                after(dve, s["cpv_mm"], b + 1)
                after(dve, s["h"], b + 1)
                for c in range(TC):
                    t = dve.scalar_tensor_tensor(csum[:, c, :], pC[:, E * c:E * c + E], rsumc[:, c:c + 1],
                                                 h[par][:, c, :], ALU.mult, ALU.add)
                t.then_inc(s["csum"], 1)
                stats(3, csum, s["csum"], b)

            def ln3(b, par):
                after(dve, s["z3t_mm"], b)
                after(dve, s["h2"], b)
                normed(3, z3, csum, b)

            def z3t(b, par):
                rest(z3T_lo, pD, z3T_hi, s["z3h"], b, s["z3l"])

            def w1(b, par):
                after(dve, s["w1_mm"], b + 1)
                dve.tensor_tensor(flat(fpre), pD[:, :], flat(b1_row), ALU.add).then_inc(s["fpre"], 1)
                after(dve, s["fpre"], b + 1)
                after(dve, s["h2"], b + 1)
                dve.scalar_tensor_tensor(flat(fsum), flat(fpre), 0.0, flat(h2[par]), ALU.max, ALU.add)\
                    .then_inc(s["fsum"], 1)
                stats(4, fsum, s["fsum"], b)

            def ln4(b, par):
                after(dve, s["z4b"], b)
                normed(4, z4, fsum, b)

            def x2sum(b, par):
                after(dve, s["z4b"], b + 1)
                after(dve, s["x1c"], b + 1)
                dve.scalar_tensor_tensor(flat(x2p), flat(z4b), 0.0, flat(x1c[par]), ALU.max, ALU.add)\
                    .then_inc(s["x2p"], 1)
                stats(5, x2p, s["x2p"], b)

            def ln5(b, par):
                after(dve, s["x2t_mm"], b)
                after(dve, s["x2b"], b)
                normed(5, x2, x2p, b)

            def x2t(b, par):
                rest(x2T_lo[par], pE, x2T_hi[par], s["x2Th"], b, s["x2Tl"])

            def lg(b, par):
                after(dve, s["lg_mm"], b + 1)
                after(dve, s["prob"], b)
                dve.tensor_tensor(flat(logit), pE[:, 0:TC * NBLK], flat(rb_row), ALU.add).then_inc(s["logit"], 1)
                after(dve, s["logit"], b + 1)
                dve.tensor_reduce(lmax[:, :], logit[:, :, :], AX.X, ALU.max, negate=True).then_inc(s["lmax"], 1)

            def tk(b, par):
                after_apart(dve, s["prob"], b + 1, own)
                for c in range(TC):
                    t = dve.max(top8[:, c, :], prob[:, c, 0:NBLK])
                t.then_inc(s["top8"], 1)
                after(dve, s["top8"], b + 1)
                dve.tensor_copy(top4[:, :, 0:TOPK], top8[:, :, 0:TOPK]).then_inc(s["top4"], 1)
                after_apart(dve, s["top4"], b + 1, own)
                for c in range(TC):
                    t = dve.match_replace(struck[:, c, :], top4[:, c, :], prob[:, c, :], -2.0)
                t.then_inc(s["struck"], 1)
                after(dve, s["struck"], b + 1)
                dve.tensor_scalar(nmask[:, :, :], struck[:, :, 0:NBLK], -1.5, -BIG, ALU.is_gt, ALU.mult)\
                    .then_inc(s["nmask"], 1)

            def hidden(f):
                def step(b, par):
                    after(dve, s_hhi[f], b + 1)
                    pair = slice(2 * f, 2 * f + 2)
                    dve.scalar_tensor_tensor(hid_lo[:, pair, :].rearrange("p a b -> p (a b)"), pH[f % 2][:, :], 0.0,
                                             hid_hi[:, pair, :].rearrange("p a b -> p (a b)").bitcast(F32),
                                             ALU.max, ALU.subtract).then_inc(s_hlo[f], 1)
                return step

            def y(b, par):
                after(dve, s["y_mm"], b + 1)
                after(dve, s["x2b"], b + 1)
                after(dve, s_ln[6], b)
                dve.tensor_tensor(flat(ysum), pH[0][:, :], flat(x2b[par]), ALU.add).then_inc(s["ysum"], 1)
                stats(6, ysum, s["ysum"], b)

            def ln6(b, par):
                if not isinstance(b, int) or b >= 2:
                    dve.wait_ge(s_st[par], loads(b, par) - 16)
                normed(6, o_sb[par], ysum, b)

            run(dve, TURN["vector"], dict(
                ret=ret_, ctx=ctx_, g=g, v=v, pt=pt, cpt=cpt, sc=sc, out1=out1, ln1=ln1, x1t=x1t, s=s_, pv=pv,
                ln2=ln2, cs=cs, cpv=cpv, ln3=ln3, z3t=z3t, w1=w1, ln4=ln4, x2sum=x2sum, ln5=ln5, x2t=x2t,
                lg=lg, tk=tk, h0=hidden(0), h1=hidden(1), h2=hidden(2), h3=hidden(3), y1=y, ln6=ln6))


def kernel(x, ctx_1024, L0_attn_basis, L0_attn_q_coeffs, L0_attn_k_coeffs, L0_attn_v_coeffs, L0_attn_o_coeffs,
           L0_attn_decay_logit, L0_attn_out_scale, L0_xattn_Wq, L0_xattn_Wk, L0_xattn_Wv, L0_xattn_Wcq, L0_xattn_Wck,
           L0_xattn_Wcv, L0_xattn_gamma, L0_xattn_beta, L0_xattn_W1, L0_xattn_b1, L0_ffn_router_w, L0_ffn_router_b,
           L0_ffn_w1, L0_ffn_b1, L0_ffn_w2, L0_ffn_b2):
    import numpy as np
    import concourse.bacc as bacc
    from concourse.bass_utils import run_bass_kernel_spmd

    def turn(a):
        return np.ascontiguousarray(np.swapaxes(np.asarray(a), -1, -2))

    def flat(a):
        return np.ascontiguousarray(np.asarray(a).reshape(-1))

    def columns(a):
        return np.ascontiguousarray(np.asarray(a).reshape(-1, P).T)

    laid = {
        "x": np.ascontiguousarray(x), "xT": turn(x), "ctxT": turn(ctx_1024), "basisT": turn(L0_attn_basis),
        "qcT": turn(L0_attn_q_coeffs), "kcT": turn(L0_attn_k_coeffs), "vcT": turn(L0_attn_v_coeffs),
        "ocT": turn(L0_attn_o_coeffs), "decay_logit": flat(L0_attn_decay_logit), "out_scale": flat(L0_attn_out_scale),
        "WqT": turn(L0_xattn_Wq), "WkT": turn(L0_xattn_Wk), "Wv": np.ascontiguousarray(L0_xattn_Wv),
        "WcqT": turn(L0_xattn_Wcq), "WckT": turn(L0_xattn_Wck), "Wcv": np.ascontiguousarray(L0_xattn_Wcv),
        "gamma": flat(L0_xattn_gamma), "beta": flat(L0_xattn_beta),
        "gammaC": columns(L0_xattn_gamma), "betaC": columns(L0_xattn_beta), "W1": np.ascontiguousarray(L0_xattn_W1),
        "b1": flat(L0_xattn_b1), "rwT": turn(L0_ffn_router_w), "rb": flat(L0_ffn_router_b), "w1T": turn(L0_ffn_w1),
        "fb1": flat(L0_ffn_b1), "w2T": turn(L0_ffn_w2), "fb2": flat(L0_ffn_b2),
    }
    nc = bacc.Bacc("TRN2", target_bir_lowering=False, num_devices=1)
    arrays, args = {}, []
    for name, a in laid.items():
        arrays[f"in_{name}"] = a
        args.append(nc.dram_tensor(f"in_{name}", a.shape, mybir.dt.from_np(a.dtype), kind="ExternalInput").ap())
    out = nc.dram_tensor("out_0", x.shape, mybir.dt.from_np(np.dtype(np.float32)), kind="ExternalOutput").ap()
    decoder_kernel(nc, *args, out)
    r = run_bass_kernel_spmd(nc, [arrays], core_ids=[0])
    return r.results[0]["out_0"]
```
